# Optimizing a Trainium2 kernel written in Bass

```python
import numpy as np
import jax
import jax.numpy as jnp

def _softmax(x, axis=-1):
    return jax.nn.softmax(x, axis=axis)

def _gelu(x):
    return jax.nn.gelu(x, approximate=True)

def _silu(x):
    return jax.nn.silu(x)

def _sigmoid(x):
    return jax.nn.sigmoid(x)

def _layernorm(x, axis=-1, eps=1e-05):
    m = jnp.mean(x, axis=axis, keepdims=True)
    v = jnp.var(x, axis=axis, keepdims=True)
    return (x - m) / jnp.sqrt(v + eps)

def _scatter_add(tgt, idx, src, axis=0):
    return tgt.at[idx].add(src)

def _segment_sum(src, seg, n):
    return jax.ops.segment_sum(src, seg, n)
kernel_name = 'mk_cond_seq_d2_seqx_r4_f7407a'

def setup_inputs(seed: int=0):
    np.random.seed(seed)
    _w = jnp.asarray

    def _rec_inputs():
        import jax
        import jax.numpy as jnp
        _rk = jax.random.key(seed)
        x = -0.0003482 + 1 * jax.random.normal(jax.random.fold_in(_rk, 1), (32, 64, 288), jnp.float32)
        _lenS = 64 - jax.random.randint(jax.random.fold_in(_rk, 7), (32,), 0, max(1, 64 // 4) + 1, jnp.int32)
        _lenS2 = 64 - jax.random.randint(jax.random.fold_in(_rk, 8), (32,), 0, max(1, 64 // 4) + 1, jnp.int32)
        cond_1152 = 0.00257642 + 1.0011 * jax.random.normal(jax.random.fold_in(_rk, 11), (32, 288), jnp.float32)
        return (x, cond_1152)
    x, cond_1152 = _rec_inputs()

    def _L0_cond_setup():
        import jax, jax.numpy as jnp
        import numpy as np
        from jax.scipy.linalg import expm
        N, D, COND_DIM = (288, 64, 288)
        B, T = (16, 256)

        def _rotation(cond, W, b):
            v = jax.nn.silu(cond) @ W.T + b
            iu, ju = jnp.triu_indices(D, k=1)
            A = jnp.zeros((cond.shape[0], D, D), dtype=v.dtype)
            A = A.at[:, iu, ju].set(v).at[:, ju, iu].set(-v)
            return expm(A)
        key = jax.random.key(seed)
        k1, k2, k3, k4, k5 = jax.random.split(key, 5)
        x = jax.random.normal(k1, (B, T, N), dtype=jnp.float32)
        cond = jax.random.normal(k2, (B, COND_DIM), dtype=jnp.float32)
        P = jax.random.normal(k3, (N, D), dtype=jnp.float32)
        n_skew = D * (D - 1) // 2
        bound = 1.0 / np.sqrt(COND_DIM)
        W = jax.random.uniform(k4, (n_skew, COND_DIM), minval=-bound, maxval=bound, dtype=jnp.float32)
        b = jax.random.uniform(k5, (n_skew,), minval=-bound, maxval=bound, dtype=jnp.float32)
        return {'x': x, 'cond': cond, 'P': P, 'W': W, 'b': b}
    _L0_cond_all = _L0_cond_setup()
    _L0_cond_in = {k: v for k, v in _L0_cond_all.items() if k in ('P', 'W', 'b')}
    del _L0_cond_all

    def _L1_cond_setup():
        import jax, jax.numpy as jnp
        import numpy as np
        B, L, C = (8, 256, 288)
        H = 16
        D = C // H
        FF = int(C * 4.0)
        EPS = 1e-06

        def _layernorm(x):
            mu = jnp.mean(x, axis=-1, keepdims=True)
            var = jnp.mean(jnp.square(x - mu), axis=-1, keepdims=True)
            return (x - mu) * jax.lax.rsqrt(var + EPS)

        def _modulate(x, shift, scale):
            return x * (1.0 + scale) + shift

        def _attention(h, W_qkv, b_qkv, W_proj, b_proj):
            b, l, c = h.shape
            qkv = h @ W_qkv + b_qkv
            qkv = qkv.reshape(b, l, 3, H, D)
            q, k, v = (qkv[:, :, 0], qkv[:, :, 1], qkv[:, :, 2])
            scale = D ** (-0.5)
            scores = jnp.einsum('blhd,bmhd->bhlm', q * scale, k)
            attn = jax.nn.softmax(scores, axis=-1)
            o = jnp.einsum('bhlm,bmhd->blhd', attn, v).reshape(b, l, c)
            return o @ W_proj + b_proj
        key = jax.random.key(seed)
        ks = jax.random.split(key, 12)
        s = 0.02
        return {'x': jax.random.normal(ks[0], (B, L, C), jnp.float32), 'c': jax.random.normal(ks[1], (B, 1, C), jnp.float32), 'W_qkv': jax.random.normal(ks[2], (C, 3 * C), jnp.float32) * s, 'b_qkv': jnp.zeros((3 * C,), jnp.float32), 'W_proj': jax.random.normal(ks[3], (C, C), jnp.float32) * s, 'b_proj': jnp.zeros((C,), jnp.float32), 'W_fc1': jax.random.normal(ks[4], (C, FF), jnp.float32) * s, 'b_fc1': jnp.zeros((FF,), jnp.float32), 'W_fc2': jax.random.normal(ks[5], (FF, C), jnp.float32) * s, 'b_fc2': jnp.zeros((C,), jnp.float32), 'W_ada': jax.random.normal(ks[6], (C, 6 * C), jnp.float32) * s, 'b_ada': jnp.zeros((6 * C,), jnp.float32)}
    _L1_cond_all = _L1_cond_setup()
    _L1_cond_in = {k: v for k, v in _L1_cond_all.items() if k in ('W_qkv', 'b_qkv', 'W_proj', 'b_proj', 'W_fc1', 'b_fc1', 'W_fc2', 'b_fc2', 'W_ada', 'b_ada')}
    del _L1_cond_all
    return {'x': x, 'cond_1152': cond_1152, 'L0_cond_P': _L0_cond_in['P'], 'L0_cond_W': _L0_cond_in['W'], 'L0_cond_b': _L0_cond_in['b'], 'L1_cond_W_qkv': _L1_cond_in['W_qkv'], 'L1_cond_b_qkv': _L1_cond_in['b_qkv'], 'L1_cond_W_proj': _L1_cond_in['W_proj'], 'L1_cond_b_proj': _L1_cond_in['b_proj'], 'L1_cond_W_fc1': _L1_cond_in['W_fc1'], 'L1_cond_b_fc1': _L1_cond_in['b_fc1'], 'L1_cond_W_fc2': _L1_cond_in['W_fc2'], 'L1_cond_b_fc2': _L1_cond_in['b_fc2'], 'L1_cond_W_ada': _L1_cond_in['W_ada'], 'L1_cond_b_ada': _L1_cond_in['b_ada']}

def reference(x, cond_1152, L0_cond_P, L0_cond_W, L0_cond_b, L1_cond_W_qkv, L1_cond_b_qkv, L1_cond_W_proj, L1_cond_b_proj, L1_cond_W_fc1, L1_cond_b_fc1, L1_cond_W_fc2, L1_cond_b_fc2, L1_cond_W_ada, L1_cond_b_ada):
    import jax
    import jax.numpy as jnp

    def _L0_cond_ref(x, cond, P, W, b):
        import jax, jax.numpy as jnp
        import numpy as np
        from jax.scipy.linalg import expm
        N, D, COND_DIM = (288, 64, 288)
        B, T = (16, 256)

        def _rotation(cond, W, b):
            v = jax.nn.silu(cond) @ W.T + b
            iu, ju = jnp.triu_indices(D, k=1)
            A = jnp.zeros((cond.shape[0], D, D), dtype=v.dtype)
            A = A.at[:, iu, ju].set(v).at[:, ju, iu].set(-v)
            return expm(A)
        U, _ = jnp.linalg.qr(P)
        R = _rotation(cond, W, b)
        z = jnp.einsum('btn,nd->btd', x, U)
        z_rot = jnp.einsum('btd,bde->bte', z, R)
        x_rot = x + jnp.einsum('btd,nd->btn', z_rot - z, U)
        return x_rot

    def _L1_cond_ref(x, c, W_qkv, b_qkv, W_proj, b_proj, W_fc1, b_fc1, W_fc2, b_fc2, W_ada, b_ada):
        import jax, jax.numpy as jnp
        import numpy as np
        B, L, C = (8, 256, 288)
        H = 16
        D = C // H
        FF = int(C * 4.0)
        EPS = 1e-06

        def _layernorm(x):
            mu = jnp.mean(x, axis=-1, keepdims=True)
            var = jnp.mean(jnp.square(x - mu), axis=-1, keepdims=True)
            return (x - mu) * jax.lax.rsqrt(var + EPS)

        def _modulate(x, shift, scale):
            return x * (1.0 + scale) + shift

        def _attention(h, W_qkv, b_qkv, W_proj, b_proj):
            b, l, c = h.shape
            qkv = h @ W_qkv + b_qkv
            qkv = qkv.reshape(b, l, 3, H, D)
            q, k, v = (qkv[:, :, 0], qkv[:, :, 1], qkv[:, :, 2])
            scale = D ** (-0.5)
            scores = jnp.einsum('blhd,bmhd->bhlm', q * scale, k)
            attn = jax.nn.softmax(scores, axis=-1)
            o = jnp.einsum('bhlm,bmhd->blhd', attn, v).reshape(b, l, c)
            return o @ W_proj + b_proj
        ada = jax.nn.silu(c) @ W_ada + b_ada
        shift_msa, scale_msa, gate_msa, shift_mlp, scale_mlp, gate_mlp = jnp.split(ada, 6, axis=-1)
        h = _modulate(_layernorm(x), shift_msa, scale_msa)
        x = x + gate_msa * _attention(h, W_qkv, b_qkv, W_proj, b_proj)
        h = _modulate(_layernorm(x), shift_mlp, scale_mlp)
        mlp = jax.nn.gelu(h @ W_fc1 + b_fc1, approximate=True) @ W_fc2 + b_fc2
        x = x + gate_mlp * mlp
        return x
    x = _L0_cond_ref(x, cond_1152, L0_cond_P, L0_cond_W, L0_cond_b)
    x = _L1_cond_ref(x, cond_1152[:, None, :], L1_cond_W_qkv, L1_cond_b_qkv, L1_cond_W_proj, L1_cond_b_proj, L1_cond_W_fc1, L1_cond_b_fc1, L1_cond_W_fc2, L1_cond_b_fc2, L1_cond_W_ada, L1_cond_b_ada)
    return x

_drawn_inputs = setup_inputs


def setup_inputs(seed=0):
    import zlib

    import numpy as np

    out = dict(_drawn_inputs(seed))
    spreads = {'L1_cond_b_qkv': (0.0, 0.8),
     'L1_cond_b_proj': (0.0, 0.349),
     'L1_cond_b_fc1': (0.0, 0.8),
     'L1_cond_b_fc2': (0.0, 0.352),
     'L1_cond_b_ada': (0.0, 0.378)}
    factors = {'L1_cond_W_qkv': 8.0, 'L1_cond_W_proj': 5.197}
    for name, (base, spread) in spreads.items():
        noise = np.random.default_rng([zlib.crc32(name.encode()), seed]).standard_normal(out[name].shape)
        drawn = base * np.exp(spread * noise) if base else spread * noise
        out[name] = jnp.asarray(drawn.astype(out[name].dtype))
    for name, factor in factors.items():
        out[name] = (out[name] * factor).astype(out[name].dtype)
    return out
```

```python
from contextlib import ExitStack
from math import factorial

import numpy as np
import concourse.bass as bass
from concourse import mybir

ALU = mybir.AluOpType
ACT = mybir.ActivationFunctionType
AX = mybir.AxisListType
F32 = mybir.dt.float32

B, L, C = 32, 64, 288
H, DH = 16, 18
D = 64
FF = 4 * C
KC, NK = 96, C // 96
NP = B // 2
G = 2
NG = NP // G
GT = G * 128
NF = FF // 128
HR = 32
VW = DH + 1
SQUARINGS = 5
TERMS = 5
LN_EPS = 1e-6
GELU_C = float(np.sqrt(2.0 / np.pi))
GELU_A = 0.044715

C_ID = 0
C_ID2 = 128
C_M1 = C_ID2 + 64
C_M2 = C_M1 + 32
C_NGT = C_M2 + 32
C_LE = C_NGT + 64
C_LV = C_LE + 64
C_UP = C_LV + 6 * 64
C_EYE = C_UP + 64
C_TINY = C_EYE + C
C_HALF = C_TINY + 1
C_ONE = C_HALF + 2
NCONST = C_ONE + 1


def constants():
    c = np.zeros((128, NCONST), np.float32)
    i = np.arange(128)
    c[i, C_ID + i] = 1
    c[i, C_ID2 + i % 64] = 1
    r, q = np.arange(32)[:, None], np.arange(32)[None, :]
    for p in range(4):
        top = p % 2 == 0
        c[32 * p:32 * p + 32, C_M1:C_M1 + 32] = (q > r) if top else -1.0 * (q < r)
        c[32 * p:32 * p + 32, C_M2:C_M2 + 32] = -1.0 * (q < r) if top else (q > r)
    i, j = np.arange(64)[:, None], np.arange(64)[None, :]
    c[:64, C_NGT:C_NGT + 64] = -1.0 * (i > j)
    c[:64, C_LE:C_LE + 64] = i <= j
    for level in range(6):
        s = 1 << level
        c[:64, C_LV + 64 * level:C_LV + 64 * level + 64] = ((i // s) % 2 == 0) & (j // s == i // s + 1)
    c[:64, C_UP:C_UP + 64] = j > i
    c[:64, C_EYE:C_EYE + C] = np.eye(64, C)
    c[:, C_TINY] = 1e-30
    c[:, C_HALF:C_HALF + 2] = -0.5
    c[:, C_ONE] = 1
    return c


def cond_block_kernel(nc, x, xT, condT, PT_, Wfold, bfold, Wada, bada_col, bada_gate, Wq, Wk, bq, bk,
                      Wv, bv, Wp, bp, Wf1, bf1, Wf2, bf2, consts, scratch, out):
    with ExitStack() as ctx:
        def sb(name, shape):
            return ctx.enter_context(nc.sbuf_tensor(name, shape, F32))

        def sem(name):
            return ctx.enter_context(nc.semaphore(name))

        ps = ctx.enter_context(nc.psum_tensor("ps", [128, 8, 512], F32))

        cst = sb("cst", [128, NCONST])
        xs = sb("xs", [128, NP, C])
        wq = sb("wq", [KC, NK, 512])
        wk = sb("wk", [KC, NK, 512])
        wv = sb("wv", [KC, NK, C])
        wp = sb("wp", [72, 4, C])
        wf1 = sb("wf1", [KC, NK, FF])
        wf2 = sb("wf2", [128, NF, C])
        bqs, bks = sb("bqs", [128, 4]), sb("bks", [128, 4])
        bvs, bps, bf2s = sb("bvs", [128, C]), sb("bps", [128, C]), sb("bf2s", [128, C])
        bf1s = sb("bf1s", [128, NF])
        gate_a = sb("gate_a", [128, NP, C])
        adaT = sb("adaT", [KC, 4, NK, B])
        bac = sb("bac", [KC, 4, NK])
        bag = sb("bag", [B, 2, C])
        gates = sb("gates", [B, 2, C])
        cT = sb("cT", [KC, NK, B])
        sT = sb("sT", [KC, NK, B])
        eT = sb("eT", [KC, NK, B])

        areaA = sb("areaA", [128, NK * NP * 128 + 768])
        xTs = areaA[0:KC, 0:NK * 2048].rearrange("p (k t) -> p k t", k=NK)
        hx = areaA[:, 0:NF * GT].rearrange("p (n t) -> p n t", n=NF)
        hg = areaA[:, NF * GT:2 * NF * GT].rearrange("p (n t) -> p n t", n=NF)
        hs = areaA[:, 2 * NF * GT:3 * NF * GT].rearrange("p (n t) -> p n t", n=NF)
        areaB = sb("areaB", [128, NK * 6 * C])
        wada = areaB[0:KC, :].rearrange("p (k n) -> p k n", k=NK)
        Pm = areaB[:, 0:2048].rearrange("p (r q m) -> p r q m", r=4, q=4)
        Pt = areaB[:, 2048:4096].rearrange("p (r q m) -> p r q m", r=4, q=4)
        oT = areaB[0:72, 4096:5120].rearrange("p (g q h t) -> p g q h t", g=G, q=2, h=2)
        areaC = sb("areaC", [128, NK * 2048 + 2048])
        wfold = areaC[0:KC, 0:NK * 2048].rearrange("p (k n) -> p k n", k=NK)
        bfs = areaC[0:B, NK * 2048:NK * 2048 + 2048]
        gate_m = areaC[:, 0:NP * C].rearrange("p (n c) -> p n c", n=NP)
        XY = areaC[:, NP * C:NP * C + 2048].rearrange("p (n s j) -> p n s j", n=NP, s=2)
        Bm = areaC[:, NP * C + 2048:NP * C + 3072].rearrange("p (n j) -> p n j", n=NP)
        areaD = sb("areaD", [128, 2048])
        Fm = areaD[:, 0:1024].rearrange("p (n j) -> p n j", n=NP)
        Am = areaD[:, 1024:2048].rearrange("p (n j) -> p n j", n=NP)
        Vb = areaD[:, 0:G * 8 * 4 * VW].rearrange("p (g n b v) -> p g n b v", g=G, n=8, b=2)
        oN = areaD[:, 1216 + 0:1216 + G * 2 * 8 * DH].rearrange("p (g b n d) -> p g b n d", g=G, b=2, n=8)
        areaE = sb("areaE", [128, 2048])
        zT = areaE[:, 0:1024].rearrange("p (n t) -> p n t", n=NP)
        wT = areaE[:, 1024:2048].rearrange("p (n t) -> p n t", n=NP)
        qT = areaE[:, 0:1024].rearrange("p (c t) -> p c t", c=4)
        kT = areaE[:, 1024:2048].rearrange("p (c t) -> p c t", c=4)
        vB = areaD[0:B, :]
        sel = areaE[0:B, :]
        Ft = areaE[:, 0:1024].rearrange("p (n j) -> p n j", n=NP)
        cI = areaE[:, 1024:1664].rearrange("p (k s j) -> p k s j", k=TERMS, s=2)
        Zl = areaE[0:D, 1664:2048].rearrange("p (l j) -> p l j", l=6)
        AT_ = sb("AT_", [128, C])
        AT = AT_[0:D, :]
        scr = sb("scr", [D, C])
        selj = sb("selj", [128, D])
        TAU = sb("TAU", [D, D])
        q_G_, q_al, q_m = sb("q_G_", [128, 1]), sb("q_al", [D, 1]), sb("q_m", [D, 1])
        q_sq, q_sg, q_nb = sb("q_sq", [D, 1]), sb("q_sg", [D, 1]), sb("q_nb", [D, 1])
        q_w, q_den, q_rd = sb("q_w", [D, 1]), sb("q_den", [D, 1]), sb("q_rd", [D, 1])
        q_G = q_G_[0:D, :]
        q_t1, q_cf = sb("q_t1", [D, 1]), sb("q_cf", [D, 1])
        tauc = sb("tauc", [D, 1])
        Vn = sb("Vn", [KC, NK, D])
        Z, Zt = sb("Z", [D, D]), sb("Zt", [D, D])
        Ztl = sb("Ztl", [D, 6, D])
        X, Xt = sb("X", [D, D]), sb("Xt", [D, D])
        P1, P2 = sb("P1", [D, D]), sb("P2", [D, D])
        tV = sb("tV", [D, D])
        Fq = sb("Fq", [D, 2, D])
        Us = sb("Us", [KC, NK, D])
        Ut = sb("Ut", [128, C])
        hT = sb("hT", [KC, NK, GT])
        xn = sb("xn", [128, G, C])
        st = sb("st", [128, G, 6])
        mv = sb("mv", [128, G, 2])
        ve = sb("ve", [128, G])
        held = sb("held", [1, 1])
        rs = sb("rs", [128, G])
        mx = sb("mx", [128, 32])
        rden = sb("rden", [128, 4, 4, 2])
        tp = sb("tp", [128, G, C])

        ident = cst[:, C_ID:C_ID + 128]
        i64 = cst[0:D, C_ID:C_ID + D]

        ld_c, ld_v, ld_ada, ld_q, ld_x, ld_xt = (sem(n) for n in ("ld_c", "ld_v", "ld_ada", "ld_q", "ld_x", "ld_xt"))
        ld_w, ld_m, ld_f = sem("ld_w"), sem("ld_m"), sem("ld_f")
        s_silu, s_exp = sem("s_silu"), sem("s_exp")
        s_vps, s_vsb, s_bounce = sem("s_vps"), sem("s_vsb"), sem("s_bounce")
        s_ada, s_adas, s_gps, s_gsb = sem("s_ada"), sem("s_adas"), sem("s_gps"), sem("s_gsb")
        s_gbc, s_gbs = sem("s_gbc"), sem("s_gbs")
        s_zero = sem("s_zero")
        s_sel, s_bc, q_dve, s_sig, q_act = (sem(n) for n in ("s_sel", "s_bc", "q_dve", "s_sig", "q_act"))
        s_pe, s_dv = sem("s_pe"), sem("s_dv")
        s_am, e_pe, e_dv = sem("s_am"), sem("e_pe"), sem("e_dv")
        s_z, s_zs, s_w, s_ws, s_xr, s_xrs = (sem(n) for n in ("s_z", "s_zs", "s_w", "s_ws", "s_xr", "s_xrs"))
        dch = sem("dch")
        a_st, a_rs, a_xn, a_T, a_mod, a_hT = (sem(n) for n in ("a_st", "a_rs", "a_xn", "a_T", "a_mod", "a_hT"))
        a_Q, a_q, a_K, a_k, a_V, a_v = (sem(n) for n in ("a_Q", "a_q", "a_K", "a_k", "a_V", "a_v"))
        a_S, a_mx, a_sub, a_exp, a_PT, a_pt = (sem(n) for n in ("a_S", "a_mx", "a_sub", "a_exp", "a_PT", "a_pt"))
        a_PV, a_rd, a_o, a_OT, a_ot, a_Y, a_y, a_res = (sem(n) for n in (
            "a_PV", "a_rd", "a_o", "a_OT", "a_ot", "a_Y", "a_y", "a_res"))
        s_vz = sem("s_vz")
        m_st, m_rs, m_xn, m_T, m_mod, m_hT = (sem(n) for n in ("m_st", "m_rs", "m_xn", "m_T", "m_mod", "m_hT"))
        m_F, m_sq, m_hx, m_in, m_th, m_g = (sem(n) for n in ("m_F", "m_sq", "m_hx", "m_in", "m_th", "m_g"))
        m_Y, m_y, m_res, m_out = (sem(n) for n in ("m_Y", "m_y", "m_res", "m_out"))

        out_t = out.rearrange("(n t) c -> t n c", t=128)
        block = ctx.enter_context(nc.Block())

        @block.sync
        def _(sp):
            sp.dma_start(cT[:], condT).then_inc(ld_c, 16)
            sp.dma_start(AT, PT_).then_inc(ld_q, 16)
            sp.dma_start(cst[:], consts).then_inc(ld_q, 16)
            for h in range(2):
                sp.dma_start(wfold[:, :, 1024 * h:1024 * h + 1024], Wfold[:, :, 1024 * h:1024 * h + 1024]).then_inc(ld_v, 16)
            sp.dma_start(bfs, bfold).then_inc(ld_v, 16)
            sp.dma_start(wada, Wada).then_inc(ld_ada, 16)
            sp.dma_start(bac[:], bada_col).then_inc(ld_ada, 16)
            sp.dma_start(bag[:], bada_gate).then_inc(ld_ada, 16)
            sp.dma_start(xTs, xT).then_inc(ld_xt, 16)
            sp.dma_start(xs[:], x.rearrange("(n t) c -> t n c", t=128)).then_inc(ld_x, 16)
            sp.wait_ge(s_vsb, 1)
            sp.dma_start(scratch, vB).then_inc(s_bounce, 16)
            sp.wait_ge(s_bounce, 16)
            rows = scratch.rearrange("(n b) (r j) -> b r n j", b=2, j=D)
            for b in range(2):
                for half in range(2):
                    at = 64 * b + 32 * half
                    sp.dma_start(Fm[at:at + 32], rows[b]).then_inc(ld_f, 16)
            with sp.Fori(0, NG) as u:
                sp.wait_ge(m_res, 2 * u + 2)
                sp.dma_start(out_t[:, bass.ds(G * u, G)], xs[:, bass.ds(G * u, G)]).then_inc(m_out, 16)
            sp.wait_ge(m_out, 16 * NG)

        @block.gpsimd
        def _(pool):
            for t, src in ((wq, Wq), (wk, Wk), (wv, Wv), (wp, Wp), (bqs, bq), (bks, bk), (bvs, bv), (bps, bp)):
                pool.dma_start(t[:], src).then_inc(ld_w, 16)
            for t, src in ((wf1, Wf1), (wf2, Wf2), (bf1s, bf1), (bf2s, bf2)):
                pool.dma_start(t[:], src).then_inc(ld_m, 16)
            pool.wait_ge(ld_q, 32)
            with pool.Fori(0, D) as j:
                pool.wait_ge(s_bc, j)
                pool.wait_ge(s_sig, j)
                pool.tensor_copy(selj[0:D], cst[0:D, bass.ds(C_ID + j, 1)].to_broadcast([D, D])).then_inc(s_sel, 1)

            def rstd(stat, done, n):
                pool.wait_ge(stat, n)
                pool.tensor_tensor(rs[:], ve[:], cst[:, C_HALF:C_HALF + G], ALU.pow).then_inc(done, 1)

            def shift(mod, done, n, which, g):
                pool.wait_ge(mod, n)
                pool.tensor_tensor(hT[:].rearrange("p k (b t) -> p k b t", b=4),
                                   hT[:].rearrange("p k (b t) -> p k b t", b=4),
                                   adaT[:, which, :, bass.ds(4 * g, 4)].unsqueeze(3).broadcast_to([KC, NK, 4, L]),
                                   ALU.add).then_inc(done, 1)

            def residual(yready, done, n, g, gate):
                pool.wait_ge(yready, n)
                pool.tensor_tensor(tp[:], tp[:], gate[:, bass.ds(G * g, G)], ALU.mult).then_inc(done, 1)
                pool.wait_ge(done, 2 * n - 1)
                pool.tensor_tensor(xs[:, bass.ds(G * g, G)], xs[:, bass.ds(G * g, G)], tp[:], ALU.add).then_inc(done, 1)

            rstd(a_st, a_rs, 1)
            shift(a_mod, a_hT, 1, 0, 0)
            rstd(a_st, a_rs, 2)

            def step(g, prev, nxt, nxt2):
                if nxt:
                    shift(a_mod, a_hT, g + 2, 0, g + 1)
                if nxt2:
                    rstd(a_st, a_rs, g + 3)
                if prev:
                    residual(a_y, a_res, g, g - 1, gate_a)

            step(0, False, True, True)
            with pool.Fori(1, NG - 2) as g:
                step(g, True, True, True)
            step(NG - 2, True, True, False)
            step(NG - 1, True, False, False)
            residual(a_y, a_res, NG, NG - 1, gate_a)

            rstd(m_st, m_rs, 1)
            shift(m_mod, m_hT, 1, 2, 0)

            def mstep(u, prev, nxt):
                if nxt:
                    rstd(m_st, m_rs, u + 2)
                if prev:
                    residual(m_y, m_res, u, u - 1, gate_m)
                if nxt:
                    shift(m_mod, m_hT, u + 2, 2, u + 1)

            mstep(0, False, True)
            with pool.Fori(1, NG - 1) as u:
                mstep(u, True, True)
            mstep(NG - 1, True, False)
            residual(m_y, m_res, NG, NG - 1, gate_m)

        @block.scalar
        def _(act):
            act.wait_ge(ld_c, 16)
            nc.scalar.activation(eT[:], cT[:], ACT.Exp, scale=-1.0).then_inc(s_exp, 1)
            act.wait_ge(ld_q, 32)
            with act.Fori(0, D) as j:
                act.wait_ge(s_sig, j + 1)
                act.wait_ge(q_dve, 13 * j)
                nc.scalar.activation(q_sq[:], ps[0:D, 7, 0:1], ACT.Sqrt, scale=4.0).then_inc(q_act, 1)
                nc.scalar.activation(q_sg[:], ps[0:D, 7, 0:1], ACT.Identity, bias=cst[0:D, C_TINY:C_TINY + 1]).then_inc(q_act, 1)

            def k_out(n):
                act.wait_ge(a_K, n)
                for c in range(4):
                    nc.scalar.activation(kT[:, c], ps[:, 6 + c // 2, 256 * (c % 2):256 * (c % 2) + 256],
                                         ACT.Identity, bias=bks[:, c:c + 1]).then_inc(a_k, 1)

            def ot_out(n):
                act.wait_ge(a_OT, n)
                for g in range(G):
                    for q in range(2):
                        src = ps[0:72, 6 + g, :].rearrange("p (b q h t) -> p q h b t", b=2, q=2, h=2)[:, q]
                        nc.scalar.activation(oT[:, g, q].rearrange("p h (b t) -> p h b t", b=2), src,
                                             ACT.Copy).then_inc(a_ot, 1)

            def exps(n):
                for r in range(4):
                    act.wait_ge(a_sub, 4 * n - 3 + r)
                    nc.scalar.activation(Pm[:, r], Pm[:, r], ACT.Exp).then_inc(a_exp, 1)

            def pt_out(n):
                for r in range(4):
                    act.wait_ge(a_PT, 4 * n - 3 + r)
                    nc.scalar.activation(Pt[:, r].rearrange("p q m -> p (q m)"), ps[:, r, :], ACT.Copy).then_inc(a_pt, 1)

            act.wait_ge(ld_w, 16 * 8)
            k_out(1)

            def step(g, prev, nxt):
                if prev:
                    ot_out(g)
                exps(g + 1)
                pt_out(g + 1)
                if nxt:
                    k_out(g + 2)

            step(0, False, True)
            with act.Fori(1, NG - 1) as g:
                step(g, True, True)
            step(NG - 1, True, False)
            ot_out(NG)

            act.wait_ge(ld_m, 16 * 4)

            def mstep(u):
                for j in range(5):
                    act.wait_ge(m_F, 5 * u + j + 1)
                    for c in range(2 * j, min(2 * j + 2, NF)):
                        ins = nc.scalar.activation(hs[:, c], ps[:, j % 4, 256 * (c % 2):256 * (c % 2) + 256],
                                                   ACT.Square, bias=bf1s[:, c:c + 1])
                    ins.then_inc(m_sq, 1)
                act.wait_ge(m_in, 2 * u + 2)
                nc.scalar.activation(hs, hs, ACT.Tanh, scale=GELU_C).then_inc(m_th, 1)

            with act.Fori(0, NG) as u:
                mstep(u)

        @block.vector
        def _(dve):
            v = nc.vector
            count = [0]

            def link(ins):
                count[0] += 1
                ins.then_inc(dch, 1)
                dve.wait_ge(dch, count[0])

            for t in (AT_, selj, q_G_):
                v.memset(t[D:128, :], 0.0).then_inc(s_zero, 1)
            dve.wait_ge(s_exp, 1)
            link(v.tensor_scalar(eT[:], eT[:], 1.0, None, ALU.add))
            link(v.reciprocal(eT[:], eT[:]))
            v.tensor_tensor(sT[:], eT[:], cT[:], ALU.mult).then_inc(s_silu, 1)
            dve.wait_ge(s_vps, 1)
            dve.wait_ge(ld_v, 48)
            v.tensor_tensor(vB, ps[0:B, 0:4, :].rearrange("p b n -> p (b n)"), bfs, ALU.add).then_inc(s_vsb, 1)
            dve.wait_ge(s_ada, 1)
            dve.wait_ge(ld_ada, 48)
            link(v.tensor_tensor(adaT[:], ps[0:KC, 4, 0:384].rearrange("p (a k b) -> p a k b", a=4, k=NK),
                                 bac[:].unsqueeze(3).broadcast_to([KC, 4, NK, B]), ALU.add))
            v.tensor_scalar(adaT[:, 1], adaT[:, 1], 1.0, None, ALU.add).then_inc(s_adas, 1)
            v.tensor_scalar(adaT[:, 3], adaT[:, 3], 1.0, None, ALU.add).then_inc(s_adas, 1)
            dve.wait_ge(ld_q, 32)
            v.tensor_copy(sel.rearrange("p (b t) -> p b t", t=L),
                          cst[0:B, C_ID:C_ID + B].unsqueeze(2).broadcast_to([B, B, L])).then_inc(s_gsb, 1)
            dve.wait_ge(s_gps, 1)
            v.tensor_tensor(gates[:], ps[0:B, 5:7, 0:C], bag[:], ALU.add).then_inc(s_gsb, 1)
            for n in range(2 * NP):
                dve.wait_ge(s_gbc, n + 1)
                v.tensor_copy((gate_a if n < NP else gate_m)[:, n % NP], ps[:, n % 4, 0:C]).then_inc(s_gbs, 1)

            dve.wait_ge(ld_q, 32)
            with dve.Fori(0, D) as j:
                bc = ps[0:D, 6, 0:C]
                bj = ps[0:D, 6, bass.ds(j, 1)]
                aj = AT[:, bass.ds(j, 1)]
                dve.wait_ge(s_bc, j + 1)
                v.tensor_tensor_reduce(out=scr[:], in0=AT, in1=bc, scale=1.0, scalar=0.0, op0=ALU.mult,
                                       op1=ALU.add, accum_out=q_G).then_inc(q_dve, 1)
                v.tensor_scalar(q_al[:], bj, 1.0, None, ALU.mult).then_inc(q_dve, 1)
                v.tensor_scalar(q_m[:], bj, 0.0, -0.5, ALU.is_ge, ALU.add).then_inc(q_dve, 1)
                dve.wait_ge(q_dve, 13 * j + 3)
                v.tensor_scalar(bj, bj, 0.0, None, ALU.mult).then_inc(q_dve, 1)
                dve.wait_ge(q_act, 2 * j + 1)
                v.tensor_scalar(q_nb[:], q_m[:], q_sq[:, 0:1], None, ALU.mult).then_inc(q_dve, 1)
                dve.wait_ge(q_dve, 13 * j + 5)
                v.tensor_scalar(q_w[:], aj, q_nb[:, 0:1], q_G[:, 0:1], ALU.mult, ALU.add).then_inc(q_dve, 1)
                dve.wait_ge(q_act, 2 * j + 2)
                v.tensor_scalar(q_den[:], q_al[:], q_nb[:, 0:1], q_sg[:, 0:1], ALU.mult, ALU.add).then_inc(q_dve, 1)
                dve.wait_ge(q_dve, 13 * j + 7)
                v.reciprocal(q_rd[:], q_den[:]).then_inc(q_dve, 1)
                v.tensor_scalar(q_t1[:], cst[0:D, bass.ds(C_ID + j, 1)], q_nb[:, 0:1], None, ALU.mult).then_inc(q_dve, 1)
                dve.wait_ge(q_dve, 13 * j + 9)
                v.tensor_scalar(aj, aj, cst[0:D, bass.ds(C_LE + j, 1)], q_t1[:, 0:1], ALU.mult, ALU.add).then_inc(q_dve, 1)
                v.tensor_scalar(q_cf[:], q_w[:], q_rd[:, 0:1], cst[0:D, bass.ds(C_NGT + j, 1)], ALU.mult, ALU.mult).then_inc(q_dve, 1)
                dve.wait_ge(q_dve, 13 * j + 11)
                v.scalar_tensor_tensor(out=AT, in0=bc, scalar=q_cf[:, 0:1], in1=AT, op0=ALU.mult,
                                       op1=ALU.add).then_inc(q_dve, 1)
                v.tensor_scalar(TAU[:, bass.ds(j, 1)], q_rd[:], 1.0, None, ALU.mult).then_inc(q_dve, 1)
            dve.wait_ge(q_dve, 13 * D)

            link(v.tensor_tensor_reduce(out=scr[:, 0:D], in0=TAU[:], in1=i64, scale=1.0, scalar=0.0, op0=ALU.mult,
                                        op1=ALU.add, accum_out=tauc[:]))
            dve.wait_ge(s_pe, 1)
            v.tensor_copy(Vn[:], ps[0:KC, 0, 0:NK * D].rearrange("p (k d) -> p k d", k=NK)).then_inc(s_dv, 1)
            link(v.tensor_scalar(tV[:], AT[:, 0:D], tauc[:, 0:1], None, ALU.mult))
            dve.wait_ge(s_pe, 2)
            link(v.tensor_scalar(Z[:], ps[0:D, 1, 0:D], tauc[:, 0:1], None, ALU.mult))
            link(v.tensor_tensor(Z[:], Z[:], cst[0:D, C_UP:C_UP + D], ALU.mult))
            v.tensor_tensor(Zl[:], Z[:].unsqueeze(1).broadcast_to([D, 6, D]),
                            cst[0:D, C_LV:C_LV + 384].rearrange("p (l j) -> p l j", l=6), ALU.mult).then_inc(s_dv, 1)
            dve.wait_ge(s_pe, 3)
            v.tensor_copy(Ztl[:], ps[0:D, 2, 0:384].rearrange("p (l j) -> p l j", l=6)).then_inc(s_dv, 1)
            v.tensor_tensor(X[:], i64, Zl[:, 0], ALU.subtract).then_inc(s_dv, 1)
            dve.wait_ge(s_dv, 3)
            v.tensor_tensor(Xt[:], i64, Ztl[:, 0], ALU.subtract).then_inc(s_dv, 1)
            for level in range(1, 6):
                dve.wait_ge(s_pe, 3 + 2 * level - 1)
                v.tensor_copy(P1[:], ps[0:D, 0, 0:D]).then_inc(s_dv, 1)
                v.tensor_copy(P2[:], ps[0:D, 0, D:2 * D]).then_inc(s_dv, 1)
                dve.wait_ge(s_pe, 3 + 2 * level)
                v.tensor_tensor(X[:], X[:], ps[0:D, 1, 0:D], ALU.subtract).then_inc(s_dv, 1)
                v.tensor_tensor(Xt[:], Xt[:], ps[0:D, 1, D:2 * D], ALU.subtract).then_inc(s_dv, 1)
            dve.wait_ge(s_pe, 14)
            v.tensor_copy(Fq[:, 0], ps[0:D, 2, 0:D]).then_inc(s_dv, 1)
            v.tensor_copy(Fq[:, 1], ps[0:D, 2, 0:D]).then_inc(s_dv, 1)
            dve.wait_ge(s_pe, 15)
            v.tensor_tensor(Us[:, 0], cst[0:KC, C_ID:C_ID + D], ps[0:KC, 3, 0:D], ALU.subtract).then_inc(s_dv, 1)
            v.tensor_scalar(Us[:, 1:3], ps[0:KC, 3, D:3 * D].rearrange("p (k d) -> p k d", k=2), -1.0, None,
                            ALU.mult).then_inc(s_dv, 1)
            v.tensor_scalar(Ut[:], ps[:, 4, 0:C], -1.0, None, ALU.mult).then_inc(s_dv, 1)
            dve.wait_ge(s_dv, 30)
            v.tensor_tensor(Ut[:, 0:D], Ut[:, 0:D], cst[:, C_ID2:C_ID2 + D], ALU.add).then_inc(s_dv, 1)

            for k in range(TERMS):
                for s in range(2):
                    coef = float((-1) ** k / factorial(2 * k + s))
                    v.tensor_scalar(cI[:, k, s], cst[:, C_ID2:C_ID2 + D], coef, None, ALU.mult).then_inc(e_dv, 1)
            dve.wait_ge(ld_f, 64)
            scaled = 1.0 / (1 << SQUARINGS)
            link(v.tensor_scalar(Fm[:], Fm[:], scaled, None, ALU.mult))
            link(v.transpose(Ft.rearrange("p n j -> p (n j)"), Fm.rearrange("p n j -> p (n j)")))
            m1 = cst[:, C_M1:C_M1 + 32].unsqueeze(1).broadcast_to([128, NP, 32])
            m2 = cst[:, C_M2:C_M2 + 32].unsqueeze(1).broadcast_to([128, NP, 32])
            link(v.tensor_tensor(XY[:, :, 0, 0:32], Fm[:, :, 0:32], m1, ALU.mult))
            link(v.tensor_tensor(XY[:, :, 1, 0:32], Ft[:, :, 0:32], m2, ALU.mult))
            link(v.tensor_tensor(XY[:, :, 0, 32:64], XY[:, :, 0, 0:32], XY[:, :, 1, 0:32], ALU.add))
            for b in range(2):
                top, low = slice(64 * b, 64 * b + 32), slice(64 * b + 32, 64 * b + 64)
                v.tensor_copy(Am[top, :, 0:32], XY[top, :, 0, 32:64]).then_inc(s_am, 1)
                v.tensor_copy(Am[top, :, 32:64], Fm[top, :, 32:64]).then_inc(s_am, 1)
                v.tensor_scalar(Am[low, :, 0:32], Ft[low, :, 32:64], -1.0, None, ALU.mult).then_inc(s_am, 1)
                v.tensor_copy(Am[low, :, 32:64], XY[low, :, 0, 32:64]).then_inc(s_am, 1)
            dve.wait_ge(s_am, 8)

            base = 2 * TERMS
            hv = lambda t, h: t[:, 8 * h:8 * h + 8]
            pb = lambda h: ps[:, 2 * h:2 * h + 2, :].rearrange("p b n -> p (b n)")
            for h in range(2):
                dve.wait_ge(e_pe, h + 1)
                v.tensor_copy(hv(Bm, h), pb(h)[:, 0:512].rearrange("p (n j) -> p n j", n=8)).then_inc(e_dv, 1)
                dve.wait_ge(e_dv, base + 4 * h + 1)
                for s in range(2):
                    k = TERMS
                    coef = float((-1) ** k / factorial(2 * k + s))
                    v.tensor_scalar(hv(XY, h)[:, :, s], hv(Bm, h), coef, None, ALU.mult).then_inc(e_dv, 1)
                dve.wait_ge(e_dv, base + 4 * h + 3)
                v.tensor_tensor(hv(XY, h), hv(XY, h), cI[:, TERMS - 1].unsqueeze(1).broadcast_to([128, 8, 2, D]),
                                ALU.add).then_inc(e_dv, 1)
            base += 8
            n_pe = 2
            for k in range(TERMS - 2, 0, -1):
                for h in range(2):
                    n_pe += 1
                    dve.wait_ge(e_pe, n_pe)
                    v.tensor_tensor(hv(XY, h), pb(h).rearrange("p (n s j) -> p n s j", n=8, s=2),
                                    cI[:, k].unsqueeze(1).broadcast_to([128, 8, 2, D]), ALU.add).then_inc(e_dv, 1)
            base += 2 * (TERMS - 2)
            for h in range(2):
                n_pe += 1
                dve.wait_ge(e_pe, n_pe)
                v.tensor_scalar(hv(XY, h), pb(h).rearrange("p (n s j) -> p n s j", n=8, s=2), 2.0, None,
                                ALU.mult).then_inc(e_dv, 1)
            base += 2
            for h in range(2):
                n_pe += 1
                dve.wait_ge(e_pe, n_pe)
                v.scalar_tensor_tensor(out=hv(XY, h)[:, :, 1], in0=hv(Am, h), scalar=2.0,
                                       in1=pb(h)[:, 0:512].rearrange("p (n j) -> p n j", n=8),
                                       op0=ALU.mult, op1=ALU.subtract).then_inc(e_dv, 1)
            base += 2
            for k in range(SQUARINGS):
                for h in range(2):
                    n_pe += 1
                    dve.wait_ge(e_pe, n_pe)
                    p4 = pb(h).rearrange("p (n s j) -> p n s j", n=8, s=2)
                    for s in range(2):
                        v.scalar_tensor_tensor(out=hv(XY, h)[:, :, s], in0=hv(XY, h)[:, :, s],
                                               scalar=4.0 if s == 0 else 2.0, in1=p4[:, :, s],
                                               op0=ALU.mult, op1=ALU.add).then_inc(e_dv, 1)
            base += 4 * SQUARINGS
            dve.wait_ge(e_dv, base)
            v.tensor_tensor(Bm[:], XY[:, :, 0], XY[:, :, 1], ALU.add).then_inc(e_dv, 1)

            for h in range(2):
                dve.wait_ge(s_z, h + 1)
                v.tensor_copy(zT[:, 8 * h:8 * h + 8], ps[:, 4 + h, :].rearrange("p (n t) -> p n t", n=8)).then_inc(s_zs, 1)
            for h in range(2):
                dve.wait_ge(s_w, h + 1)
                v.tensor_scalar(wT[:, 8 * h:8 * h + 8], ps[:, 6 + h, :].rearrange("p (n t) -> p n t", n=8),
                                0.5, None, ALU.mult).then_inc(s_ws, 1)
            dve.wait_ge(ld_x, 16)
            for n in range(NP):
                dve.wait_ge(s_xr, n + 1)
                v.tensor_tensor(xs[:, n], xs[:, n], ps[:, n % 4, 0:C], ALU.add).then_inc(s_xrs, 1)

            v.memset(areaD[:, 0:G * 8 * 4 * VW], 0.0).then_inc(s_vz, 1)
            dve.wait_ge(s_vz, 1)
            for b in range(2):
                v.memset(Vb[64 * b:64 * b + 64, :, :, b].rearrange("p g n (h v) -> p (g n) h v", v=VW)[:, :, :, DH], 1.0
                         ).then_inc(s_vz, 1)
            dve.wait_ge(ld_w, 16 * 8)
            dve.wait_ge(s_xrs, NP)

            def stats(stat, rstd, xnd, n, g):
                for t in range(G):
                    v.bn_stats(st[:, t], xs[:, bass.ds(G * g + t, 1)].rearrange("p a c -> p (a c)")).then_inc(stat[1], 1)
                dve.wait_ge(stat[1], 5 * n - 3)
                v.memset(held[:], 0.0).then_inc(stat[1], 1)
                for t in range(G):
                    v.bn_aggr(mv[:, t], st[:, t]).then_inc(stat[1], 1)
                dve.wait_ge(stat[1], 5 * n)
                v.tensor_scalar(ve[:], mv[:, :, 1], LN_EPS, None, ALU.add).then_inc(stat[0], 1)
                dve.wait_ge(rstd, n)
                for t in range(G):
                    v.tensor_scalar(xn[:, t], xs[:, bass.ds(G * g + t, 1)].rearrange("p a c -> p (a c)"),
                                    mv[:, t, 0:1], rs[:, t:t + 1], ALU.subtract, ALU.mult).then_inc(xnd, 1)

            def scale(T, mod, n, which, g):
                dve.wait_ge(T, n)
                src = ps[0:KC, 4:6, :].rearrange("p b n -> p (b n)")[:, 0:NK * GT].rearrange(
                    "p (k b t) -> p k b t", k=NK, b=4)
                v.tensor_tensor(hT[:].rearrange("p k (b t) -> p k b t", b=4), src,
                                adaT[:, which, :, bass.ds(4 * g, 4)].unsqueeze(3).broadcast_to([KC, NK, 4, L]),
                                ALU.mult).then_inc(mod, 1)

            def q_out(n):
                dve.wait_ge(a_Q, n)
                for c in range(4):
                    v.tensor_scalar(qT[:, c], ps[:, 4 + c // 2, 256 * (c % 2):256 * (c % 2) + 256], bqs[:, c:c + 1],
                                    float(DH) ** -0.5, ALU.add, ALU.mult).then_inc(a_q, 1)

            def v_out(n):
                dve.wait_ge(a_V, n)
                for g in range(G):
                    for b in range(2):
                        at = slice(64 * b, 64 * b + 64)
                        v.tensor_tensor(
                            Vb[at, g, :, b].rearrange("p n (h v) -> p n h v", v=VW)[:, :, :, 0:DH],
                            ps[at, 6 + g, 0:C].rearrange("p (n h d) -> p n h d", n=8, h=2),
                            bvs[at, :].rearrange("p (n h d) -> p n h d", n=8, h=2), ALU.add).then_inc(a_v, 1)

            def maxima(n):
                dve.wait_ge(a_S, n)
                v.tensor_reduce(mx[:].rearrange("p (r q) -> p r q", r=4), ps[:, 0:4, :].rearrange("p r (q m) -> p r q m", m=L),
                                AX.X, ALU.max).then_inc(a_mx, 1)
                dve.wait_ge(a_mx, n)
                for r in range(4):
                    v.tensor_tensor(Pm[:, r].rearrange("p q (b m) -> p (q b) m", m=L), ps[:, r, :].rearrange("p (q m) -> p q m", m=L),
                                    mx[:, 8 * r:8 * r + 8].unsqueeze(2).broadcast_to([128, 8, L]),
                                    ALU.subtract).then_inc(a_sub, 1)

            def norm(n):
                for g in range(G):
                    dve.wait_ge(a_PV, 2 * n - 1 + g)
                    for h in range(2):
                        at = slice(64 * h, 64 * h + 64)
                        src = ps[at, 4 + 2 * g:6 + 2 * g, 0:304].rearrange("p q (r b v) -> p q r b v", r=4, b=2)
                        v.reciprocal(rden[at, 2 * g:2 * g + 2], src[:, :, :, :, h * VW + DH]).then_inc(a_rd, 1)
                    dve.wait_ge(a_rd, 4 * n - 2 + 2 * g)
                    for h in range(2):
                        at = slice(64 * h, 64 * h + 64)
                        for q in range(2):
                            src = ps[at, 4 + 2 * g + q, 0:304].rearrange("p (r b v) -> p r b v", r=4, b=2)
                            v.tensor_tensor(
                                oN[at, g, :, 4 * q:4 * q + 4].rearrange("p b r d -> p r b d"),
                                src[:, :, :, h * VW:h * VW + DH],
                                rden[at, 2 * g + q].unsqueeze(3).broadcast_to([64, 4, 2, DH]),
                                ALU.mult).then_inc(a_o, 1)

            def proj_out(Y, y, res, n, bank, bias, half):
                dve.wait_ge(res, 2 * n - 2)
                for t in range(G):
                    dve.wait_ge(Y, G * n - 1 + t)
                if half is None:
                    v.tensor_tensor(tp[:], ps[:, bank:bank + 2, 0:C], bias[:].unsqueeze(1).broadcast_to([128, G, C]),
                                    ALU.add).then_inc(y, 1)
                else:
                    v.scalar_tensor_tensor(out=tp[:], in0=ps[:, bank:bank + 2, 0:C], scalar=half,
                                           in1=bias[:].unsqueeze(1).broadcast_to([128, G, C]),
                                           op0=ALU.mult, op1=ALU.add).then_inc(y, 1)

            A_ST = (a_st, dch2 := sem("a_bn"))
            stats(A_ST, a_rs, a_xn, 1, 0)
            scale(a_T, a_mod, 1, 1, 0)
            stats(A_ST, a_rs, a_xn, 2, 1)
            q_out(1)
            v_out(1)

            def step(g, prev, nxt, nxt2):
                if nxt:
                    dve.wait_ge(a_V, g + 1)
                    scale(a_T, a_mod, g + 2, 1, g + 1)
                if nxt2:
                    stats(A_ST, a_rs, a_xn, g + 3, g + 2)
                maxima(g + 1)
                if prev:
                    proj_out(a_Y, a_y, a_res, g, 6, bps, None)
                if nxt:
                    q_out(g + 2)
                norm(g + 1)
                if nxt:
                    v_out(g + 2)

            step(0, False, True, True)
            with dve.Fori(1, NG - 2) as g:
                step(g, True, True, True)
            step(NG - 2, True, True, False)
            step(NG - 1, True, False, False)
            proj_out(a_Y, a_y, a_res, NG, 6, bps, None)

            dve.wait_ge(a_res, 2 * NG)
            dve.wait_ge(ld_m, 16 * 4)
            M_ST = (m_st, sem("m_bn"))
            stats(M_ST, m_rs, m_xn, 1, 0)
            scale(m_T, m_mod, 1, 3, 0)

            def mstep(u, prev, nxt):
                for j in range(5):
                    dve.wait_ge(m_sq, 5 * u + j + 1)
                    for c in range(2 * j, min(2 * j + 2, NF)):
                        ins = v.tensor_scalar(hx[:, c], ps[:, j % 4, 256 * (c % 2):256 * (c % 2) + 256],
                                              bf1s[:, c:c + 1], None, ALU.add)
                        ins.then_inc(m_hx, 1)
                v.tensor_scalar(hs[:], hs[:], GELU_A, 1.0, ALU.mult, ALU.add).then_inc(m_in, 1)
                dve.wait_ge(m_in, 2 * u + 1)
                dve.wait_ge(m_hx, 9 * u + 9)
                v.tensor_tensor(hs[:], hs[:], hx[:], ALU.mult).then_inc(m_in, 1)
                if nxt:
                    stats(M_ST, m_rs, m_xn, u + 2, u + 1)
                if prev:
                    proj_out(m_Y, m_y, m_res, u, 6, bf2s, 0.5)
                dve.wait_ge(m_th, u + 1)
                v.scalar_tensor_tensor(out=hg[:], in0=hs[:], scalar=1.0, in1=hx[:], op0=ALU.add,
                                       op1=ALU.mult).then_inc(m_g, 1)
                if nxt:
                    scale(m_T, m_mod, u + 2, 3, u + 1)

            mstep(0, False, True)
            with dve.Fori(1, NG - 1) as u:
                mstep(u, True, True)
            mstep(NG - 1, True, False)
            proj_out(m_Y, m_y, m_res, NG, 6, bf2s, 0.5)

        @block.tensor
        def _(pe):
            def mm(out_, lhsT, rhs, first=True, last=True):
                return nc.tensor.matmul(out_, lhsT, rhs, start=first, stop=last)

            pe.wait_ge(s_silu, 1)
            pe.wait_ge(ld_v, 48)
            for n in range(4):
                for k in range(NK):
                    ins = mm(ps[0:B, n, :], sT[:, k], wfold[:, k, 512 * n:512 * n + 512], k == 0, k == NK - 1)
            ins.then_inc(s_vps, 1)
            pe.wait_ge(ld_ada, 48)
            for a, part in enumerate((0, 1, 3, 4)):
                for c in range(NK):
                    for k in range(NK):
                        col = part * C + c * KC
                        ins = mm(ps[0:KC, 4, 32 * (NK * a + c):32 * (NK * a + c) + 32], wada[:, k, col:col + KC],
                                 sT[:, k], k == 0, k == NK - 1)
            ins.then_inc(s_ada, 1)
            for n, part in enumerate((2, 5)):
                for k in range(NK):
                    ins = mm(ps[0:B, 5 + n, 0:C], sT[:, k], wada[:, k, part * C:part * C + C], k == 0, k == NK - 1)
            ins.then_inc(s_gps, 1)
            pe.wait_ge(s_gsb, 2)
            pe.wait_ge(s_vsb, 1)
            pe.wait_ge(ld_q, 32)
            for n in range(2 * NP):
                if n >= 4:
                    pe.wait_ge(s_gbs, n - 3)
                p = n % NP
                mm(ps[:, n % 4, 0:C], sel[:, 128 * p:128 * p + 128], gates[:, n // NP]).then_inc(s_gbc, 1)

            pe.wait_ge(s_zero, 3)
            with pe.Fori(0, D) as j:
                pe.wait_ge(s_sel, j + 1)
                pe.wait_ge(q_dve, 13 * j)
                mm(ps[0:D, 6, 0:C], selj[:], AT_[:]).then_inc(s_bc, 1)
                pe.wait_ge(q_dve, 13 * j + 1)
                pe.wait_ge(q_act, 2 * j)
                mm(ps[0:D, 7, 0:1], selj[:], q_G_[:]).then_inc(s_sig, 1)

            pe.wait_ge(q_dve, 13 * D)
            pe.wait_ge(s_gbs, 2 * NP)
            for k in range(NK):
                ins = nc.tensor.transpose(ps[0:KC, 0, D * k:D * k + D], AT[:, KC * k:KC * k + KC], i64)
            ins.then_inc(s_pe, 1)
            pe.wait_ge(s_dv, 1)
            for k in range(NK):
                ins = mm(ps[0:D, 1, 0:D], Vn[:, k], Vn[:, k], k == 0, k == NK - 1)
            ins.then_inc(s_pe, 1)
            pe.wait_ge(s_dv, 2)
            for level in range(6):
                ins = nc.tensor.transpose(ps[0:D, 2, D * level:D * level + D], Zl[:, level], i64)
            ins.then_inc(s_pe, 1)
            for level in range(1, 6):
                pe.wait_ge(s_dv, 5 + 4 * (level - 1))
                mm(ps[0:D, 0, 0:D], Ztl[:, level], X[:])
                mm(ps[0:D, 0, D:2 * D], Zl[:, level], Xt[:]).then_inc(s_pe, 1)
                pe.wait_ge(s_dv, 5 + 4 * (level - 1) + 2)
                mm(ps[0:D, 1, 0:D], Xt[:], P1[:])
                mm(ps[0:D, 1, D:2 * D], X[:], P2[:]).then_inc(s_pe, 1)
            pe.wait_ge(s_dv, 25)
            mm(ps[0:D, 2, 0:D], Xt[:], tV[:]).then_inc(s_pe, 1)
            pe.wait_ge(s_dv, 27)
            for k in range(NK):
                mm(ps[0:KC, 3, D * k:D * k + D], AT[:, KC * k:KC * k + KC], Fq[:, 0])
            mm(ps[:, 4, 0:C], Fq[:].rearrange("p a b -> p (a b)"), AT).then_inc(s_pe, 1)

            def products(left, right, width, h):
                for n in range(8):
                    for b in range(2):
                        at = slice(64 * b, 64 * b + 64)
                        o = ps[at, 2 * h + n * width // 512, n * width % 512:n * width % 512 + width]
                        ins = mm(o, left[at, 8 * h + n], right[at, 8 * h + n])
                ins.then_inc(e_pe, 1)

            done = 2 * TERMS
            pe.wait_ge(s_am, 8)
            pe.wait_ge(s_dv, 31)
            for h in range(2):
                products(Am, Am, D, h)
            for k in range(TERMS - 2, -1, -1):
                for h in range(2):
                    pe.wait_ge(e_dv, done + (4 * h + 4 if k == TERMS - 2 else h + 1))
                    products(Bm, XY, 2 * D, h)
                done += 8 if k == TERMS - 2 else 2
            for h in range(2):
                pe.wait_ge(e_dv, done + h + 1)
                products(Am, XY[:, :, 1], D, h)
            done += 2
            for k in range(SQUARINGS):
                for h in range(2):
                    pe.wait_ge(e_dv, done + (h + 1 if k == 0 else 2 * h + 2))
                    products(XY[:, :, 0], XY, 2 * D, h)
                done += 2 if k == 0 else 4
            done += 4

            pe.wait_ge(ld_xt, 16)
            for h in range(2):
                for b in range(2):
                    for k in range(NK):
                        rhs = xTs[:, k].rearrange("p (n b t) -> p b n t", b=2, t=L)[:, b, 8 * h:8 * h + 8]
                        ins = mm(ps[64 * b:64 * b + 64, 4 + h, :], Us[:, k], rhs, k == 0, k == NK - 1)
                ins.then_inc(s_z, 1)
            pe.wait_ge(e_dv, done + 1)
            for h in range(2):
                pe.wait_ge(s_zs, h + 1)
                for n in range(8 * h, 8 * h + 8):
                    for b in range(2):
                        at = slice(64 * b, 64 * b + 64)
                        ins = mm(ps[at, 6 + h, L * (n % 8):L * (n % 8) + L], Bm[at, n], zT[at, n])
                ins.then_inc(s_w, 1)
            for n in range(NP):
                pe.wait_ge(s_ws, n // 8 + 1)
                if n >= 4:
                    pe.wait_ge(s_xrs, n - 3)
                for b in range(2):
                    at = slice(64 * b, 64 * b + 64)
                    ins = mm(ps[at, n % 4, 0:C], wT[at, n], Ut[at])
                ins.then_inc(s_xr, 1)

            def turn(xnd, T, n):
                pe.wait_ge(xnd, G * n)
                flat = ps[0:KC, 4:6, :].rearrange("p b n -> p (b n)")
                for k in range(NK):
                    for t in range(G):
                        ins = nc.tensor.transpose(flat[:, GT * k + 128 * t:GT * k + 128 * t + 128],
                                                  xn[:, t, KC * k:KC * k + KC], ident)
                ins.then_inc(T, 1)

            def qk(w, bank, ready, n):
                for c in range(4):
                    for k in range(NK):
                        ins = mm(ps[:, bank + c // 2, 256 * (c % 2):256 * (c % 2) + 256],
                                 w[:, k, 128 * c:128 * c + 128], hT[:, k], k == 0, k == NK - 1)
                ins.then_inc(ready, 1)

            def values(n):
                for t in range(G):
                    for k in range(NK):
                        ins = mm(ps[:, 6 + t, 0:C], hT[:, k, 128 * t:128 * t + 128], wv[:, k], k == 0, k == NK - 1)
                ins.then_inc(a_V, 1)

            def scores(n):
                pe.wait_ge(a_q, 4 * n)
                pe.wait_ge(a_k, 4 * n)
                for t in range(G):
                    for q in range(2):
                        for b in range(2):
                            tok = slice(128 * t + 64 * b, 128 * t + 64 * b + 64)
                            at = 256 * t + 128 * q + 64 * b
                            for h in range(2):
                                for r in range(4):
                                    ins = mm(ps[64 * h:64 * h + 64, r, at:at + L],
                                             qT[HR * r:HR * r + DH, 2 * q + h, tok],
                                             kT[HR * r:HR * r + DH, 2 * q + h, tok])
                ins.then_inc(a_S, 1)

            def turn_out(n):
                pe.wait_ge(a_o, 8 * n)
                for g in range(G):
                    for b in range(2):
                        for q in range(2):
                            ins = nc.tensor.transpose(ps[0:72, 6 + g, 256 * b + 128 * q:256 * b + 128 * q + 128],
                                                      oN[:, g, b, 4 * q:4 * q + 4].rearrange("p r d -> p (r d)"), ident)
                ins.then_inc(a_OT, 1)

            def project(n):
                pe.wait_ge(a_ot, 4 * n)
                for t in range(G):
                    for c in range(4):
                        ins = mm(ps[:, 6 + t, 0:C], oT[:, t, c // 2, c % 2], wp[:, c], c == 0, c == 3)
                    ins.then_inc(a_Y, 1)

            def turn_p(n):
                for r in range(4):
                    pe.wait_ge(a_exp, 4 * n - 3 + r)
                    for q in range(4):
                        ins = nc.tensor.transpose(ps[:, r, 128 * q:128 * q + 128], Pm[:, r, q], ident)
                    ins.then_inc(a_PT, 1)

            def pv(n):
                pe.wait_ge(a_pt, 4 * n)
                pe.wait_ge(a_v, 4 * n)
                for g in range(G):
                    for q in range(2):
                        for r in range(4):
                            ins = mm(ps[:, 4 + 2 * g + q, 4 * VW * r:4 * VW * r + 4 * VW], Pt[:, r, 2 * g + q],
                                     Vb[:, g, 4 * q + r].rearrange("p b v -> p (b v)"))
                    ins.then_inc(a_PV, 1)

            pe.wait_ge(s_vz, 3)
            pe.wait_ge(ld_w, 16 * 8)
            turn(a_xn, a_T, 1)
            pe.wait_ge(a_hT, 1)
            qk(wq, 4, a_Q, 1)
            qk(wk, 6, a_K, 1)
            pe.wait_ge(a_q, 4)
            turn(a_xn, a_T, 2)
            pe.wait_ge(a_k, 4)
            values(1)

            def step(g, prev, nxt, nxt2):
                scores(g + 1)
                if prev:
                    pe.wait_ge(a_v, 4 * (g + 1))
                    turn_out(g)
                    project(g)
                if nxt:
                    pe.wait_ge(a_hT, g + 2)
                    qk(wq, 4, a_Q, g + 2)
                turn_p(g + 1)
                if nxt:
                    if prev:
                        pe.wait_ge(a_y, g)
                    qk(wk, 6, a_K, g + 2)
                    pe.wait_ge(a_q, 4 * (g + 2))
                    pe.wait_ge(a_k, 4 * (g + 2))
                elif prev:
                    pe.wait_ge(a_y, g)
                pv(g + 1)
                if nxt2:
                    pe.wait_ge(a_o, 8 * g + 4)
                    turn(a_xn, a_T, g + 3)
                if nxt:
                    pe.wait_ge(a_o, 8 * g + 8)
                    values(g + 2)
                    
            step(0, False, True, True)
            with pe.Fori(1, NG - 2) as g:
                step(g, True, True, True)
            step(NG - 2, True, True, False)
            step(NG - 1, True, False, False)
            turn_out(NG)
            project(NG)

            def hidden(u):
                pe.wait_ge(m_hT, u + 1)
                for j in range(5):
                    if j == 4:
                        pe.wait_ge(m_hx, 9 * u + 2)
                    for c in range(2 * j, min(2 * j + 2, NF)):
                        for k in range(NK):
                            ins = mm(ps[:, j % 4, 256 * (c % 2):256 * (c % 2) + 256],
                                     wf1[:, k, 128 * c:128 * c + 128], hT[:, k], k == 0, k == NK - 1)
                    ins.then_inc(m_F, 1)

            def down(n):
                pe.wait_ge(m_g, n)
                for t in range(G):
                    for c in range(NF):
                        ins = mm(ps[:, 6 + t, 0:C], hg[:, c, 128 * t:128 * t + 128], wf2[:, c], c == 0, c == NF - 1)
                    ins.then_inc(m_Y, 1)

            pe.wait_ge(ld_m, 16 * 4)
            pe.wait_ge(a_y, NG)
            turn(m_xn, m_T, 1)

            def mstep(u, prev, nxt):
                if prev:
                    pe.wait_ge(m_hx, 9 * u)
                hidden(u)
                if nxt:
                    turn(m_xn, m_T, u + 2)
                if prev:
                    down(u)

            mstep(0, False, True)
            with pe.Fori(1, NG - 1) as u:
                mstep(u, True, True)
            mstep(NG - 1, True, False)
            down(NG)


def kernel(x, cond_1152, L0_cond_P, L0_cond_W, L0_cond_b, L1_cond_W_qkv, L1_cond_b_qkv, L1_cond_W_proj,
           L1_cond_b_proj, L1_cond_W_fc1, L1_cond_b_fc1, L1_cond_W_fc2, L1_cond_b_fc2, L1_cond_W_ada, L1_cond_b_ada):
    import concourse.bacc as bacc
    from concourse.bass_utils import run_bass_kernel_spmd

    def chunks(a):
        return a.reshape(NK, KC, -1).transpose(1, 0, 2)

    def rep(a, n):
        return np.tile(np.asarray(a)[None], (n,) + (1,) * np.asarray(a).ndim)

    def heads(a):
        a = a.reshape(-1, 2, 4, 2, DH).transpose(0, 1, 3, 2, 4)
        padded = np.zeros(a.shape[:-1] + (HR,), np.float32)
        padded[..., :DH] = a
        return padded.reshape(padded.shape[0], 512)

    tokens = np.asarray(x).reshape(B * L, C)
    Wr, br = np.asarray(L0_cond_W), np.asarray(L0_cond_b)
    packed = np.zeros((D, D), np.int64)
    packed[np.triu_indices(D, 1)] = np.arange(D * (D - 1) // 2)
    fold_w = np.zeros((32, D, C), np.float32)
    fold_b = np.zeros((32, D), np.float32)
    for r in range(32):
        for c in range(D):
            if c != r:
                k = packed[r, c] if c > r else packed[32 + c, 32 + r]
                fold_w[r, c], fold_b[r, c] = Wr[k], br[k]
    Wqkv, bqkv = np.asarray(L1_cond_W_qkv), np.asarray(L1_cond_b_qkv)
    bada = np.asarray(L1_cond_b_ada).reshape(6, C)
    arrays = {
        "x": tokens,
        "xT": chunks(tokens.T),
        "condT": chunks(np.asarray(cond_1152).T),
        "PT": np.asarray(L0_cond_P).T,
        "Wfold": chunks(fold_w.reshape(2048, C).T),
        "bfold": rep(fold_b.reshape(2048), B),
        "Wada": chunks(np.asarray(L1_cond_W_ada)),
        "bada_col": bada[[0, 1, 3, 4]].reshape(4, NK, KC).transpose(2, 0, 1),
        "bada_gate": rep(bada[[2, 5]], B),
        "Wq": chunks(heads(Wqkv[:, 0:C])),
        "Wk": chunks(heads(Wqkv[:, C:2 * C])),
        "bq": heads(bqkv[None, 0:C]).reshape(4, 128).T,
        "bk": heads(bqkv[None, C:2 * C]).reshape(4, 128).T,
        "Wv": chunks(Wqkv[:, 2 * C:]),
        "bv": rep(bqkv[2 * C:], 128),
        "Wp": np.asarray(L1_cond_W_proj).reshape(2, 4, 2, DH, C).transpose(1, 3, 0, 2, 4).reshape(72, 4, C),
        "bp": rep(L1_cond_b_proj, 128),
        "Wf1": chunks(np.asarray(L1_cond_W_fc1)),
        "bf1": np.asarray(L1_cond_b_fc1).reshape(NF, 128).T,
        "Wf2": np.asarray(L1_cond_W_fc2).reshape(NF, 128, C).transpose(1, 0, 2),
        "bf2": rep(L1_cond_b_fc2, 128),
        "consts": constants(),
    }
    nc = bacc.Bacc("TRN2", target_bir_lowering=False, num_devices=1)
    feed, args = {}, []
    for name, a in arrays.items():
        a = np.ascontiguousarray(a)
        feed[f"in_{name}"] = a
        args.append(nc.dram_tensor(f"in_{name}", a.shape, F32, kind="ExternalInput").ap())
    args.append(nc.dram_tensor("skew_scratch", (B, 2048), F32, kind="Internal").ap())
    args.append(nc.dram_tensor("out", (B * L, C), F32, kind="ExternalOutput").ap())
    cond_block_kernel(nc, *args)
    r = run_bass_kernel_spmd(nc, [feed], core_ids=[0])
    return r.results[0]["out"].reshape(B, L, C)
```

```python
from contextlib import ExitStack
from math import factorial

import numpy as np
import concourse.bass as bass
from concourse import mybir

ALU = mybir.AluOpType
ACT = mybir.ActivationFunctionType
AX = mybir.AxisListType
F32 = mybir.dt.float32

B, L, C = 32, 64, 288
H, DH = 16, 18
D = 64
FF = 4 * C
KC, NK = 96, C // 96
NP = B // 2
G = 2
NG = NP // G
GT = G * 128
NF = FF // 128
HR = 32
VW = DH + 1
SQUARINGS = 5
TERMS = 5
LN_EPS = 1e-6
GELU_C = float(np.sqrt(2.0 / np.pi))
GELU_A = 0.044715

C_ID = 0
C_ID2 = 128
C_M1 = C_ID2 + 64
C_M2 = C_M1 + 32
C_NGT = C_M2 + 32
C_LE = C_NGT + 64
C_LV = C_LE + 64
C_UP = C_LV + 6 * 64
C_EYE = C_UP + 64
C_TINY = C_EYE + C
C_HALF = C_TINY + 1
C_4I = C_HALF + 2
C_2I = C_4I + 128
C_N2I = C_2I + 128
C_ONES = C_N2I + 128
NCONST = C_ONES + B


E_STAGES = 1 + (TERMS - 1) + 1 + SQUARINGS
E_FIRST = 20
QR_STEPS = 1 + 32 * 13 + 32 * 12 - 1
FOLD_AT = 11


def E_ACT(stage, q):
    return 3 * (q + 1) if stage == 0 else 12 + 4 * (stage - 1) + q + 1


def constants():
    c = np.zeros((128, NCONST), np.float32)
    i = np.arange(128)
    c[i, C_ID + i] = 1
    c[i, C_ID2 + i % 64] = 1
    r, q = np.arange(32)[:, None], np.arange(32)[None, :]
    for p in range(4):
        top = p % 2 == 0
        c[32 * p:32 * p + 32, C_M1:C_M1 + 32] = (q > r) if top else -1.0 * (q < r)
        c[32 * p:32 * p + 32, C_M2:C_M2 + 32] = -1.0 * (q < r) if top else (q > r)
    i, j = np.arange(64)[:, None], np.arange(64)[None, :]
    c[:64, C_NGT:C_NGT + 64] = -1.0 * (i > j)
    c[:64, C_LE:C_LE + 64] = i <= j
    for level in range(6):
        s = 1 << level
        c[:64, C_LV + 64 * level:C_LV + 64 * level + 64] = ((i // s) % 2 == 0) & (j // s == i // s + 1)
    c[:64, C_UP:C_UP + 64] = j > i
    c[:64, C_EYE:C_EYE + C] = np.eye(64, C)
    c[:, C_TINY] = 1e-30
    c[:, C_HALF:C_HALF + 2] = -0.5
    for at, value in ((C_4I, 4), (C_2I, 2), (C_N2I, -2)):
        c[np.arange(128), at + np.arange(128)] = value
    c[:, C_ONES:] = 1
    return c


def cond_block_kernel(nc, x, xT, condT, PT_, Wfold, bfold, Wada, bada_col, bada_gate, Wq, Wk, bq, bk,
                      Wv, bv, Wp, bp, Wf1, bf1, Wf2, bf2, consts, scratch, out):
    with ExitStack() as ctx:
        def sb(name, shape):
            return ctx.enter_context(nc.sbuf_tensor(name, shape, F32))

        def sem(name):
            return ctx.enter_context(nc.semaphore(name))

        ps = ctx.enter_context(nc.psum_tensor("ps", [128, 8, 512], F32))

        cst = sb("cst", [128, NCONST])
        xs = sb("xs", [128, NP, C])
        wq = sb("wq", [KC, NK, 512])
        wk = sb("wk", [KC, NK, 512])
        wv = sb("wv", [KC, NK, C])
        wp = sb("wp", [72, 4, C])
        wf1 = sb("wf1", [KC, NK, FF])
        wf2 = sb("wf2", [128, NF, C])
        bqs, bks = sb("bqs", [128, 4]), sb("bks", [128, 4])
        bvs, bps, bf2s = sb("bvs", [128, C]), sb("bps", [128, C]), sb("bf2s", [128, C])
        bf1s = sb("bf1s", [128, NF])
        gate_a = sb("gate_a", [128, NP, C])
        adaT = sb("adaT", [KC, 4, NK, B])
        bac = sb("bac", [KC, 4, NK])
        bag = sb("bag", [1, 2, C])
        gates = sb("gates", [B, 2, C])
        cT = sb("cT", [KC, NK, B])
        sT = sb("sT", [KC, NK, B])
        eT = sb("eT", [KC, NK, B])

        areaA = sb("areaA", [128, NK * NP * 128 + 768])
        xTs = areaA[0:KC, 0:NK * 2048].rearrange("p (k t) -> p k t", k=NK)
        hx = areaA[:, 0:NF * GT].rearrange("p (n t) -> p n t", n=NF)
        hg = areaA[:, NF * GT:2 * NF * GT].rearrange("p (n t) -> p n t", n=NF)
        hs = areaA[:, 2 * NF * GT:3 * NF * GT].rearrange("p (n t) -> p n t", n=NF)
        areaB = sb("areaB", [128, NK * 6 * C])
        wada = areaB[0:KC, :].rearrange("p (k n) -> p k n", k=NK)
        Pm = areaB[:, 0:2048].rearrange("p (t q r b m) -> p t q r b m", t=G, q=2, r=4, b=2)
        Pt = areaB[:, 2048:4096].rearrange("p (t q r m) -> p t q r m", t=G, q=2, r=4)
        oT = areaB[0:72, 4096:5120].rearrange("p (g q h t) -> p g q h t", g=G, q=2, h=2)
        areaC = sb("areaC", [128, NK * 2048 + 2048])
        wfold = areaC[0:KC, 0:NK * 2048].rearrange("p (k n) -> p k n", k=NK)
        bfs = areaC[0:1, NK * 2048:NK * 2048 + 2048]
        gate_m = areaC[:, 0:NP * C].rearrange("p (n c) -> p n c", n=NP)
        XY = areaC[:, NP * C:NP * C + 2048].rearrange("p (n s j) -> p n s j", n=NP, s=2)
        Bm = areaC[:, NP * C + 2048:NP * C + 3072].rearrange("p (n j) -> p n j", n=NP)
        areaD = sb("areaD", [128, 2048])
        Fm = areaD[:, 0:1024].rearrange("p (n j) -> p n j", n=NP)
        Am = areaD[:, 1024:2048].rearrange("p (n j) -> p n j", n=NP)
        Vb = areaD[:, 0:G * 8 * 4 * VW].rearrange("p (g n b v) -> p g n b v", g=G, n=8, b=2)
        oN = areaD[:, 1216 + 0:1216 + G * 2 * 8 * DH].rearrange("p (g b n d) -> p g b n d", g=G, b=2, n=8)
        areaE = sb("areaE", [128, 2048])
        zT = areaE[:, 0:1024].rearrange("p (n t) -> p n t", n=NP)
        wT = areaE[:, 1024:2048].rearrange("p (n t) -> p n t", n=NP)
        qT = areaE[:, 0:1024].rearrange("p (c t) -> p c t", c=4)
        kD = [a.rearrange("p (e r m) -> p e r m", e=2 * G, r=4)
              for a in (areaC[:, NP * C:NP * C + 1024], areaC[:, NP * C + 1024:NP * C + 2048],
                        areaC[:, NP * C + 2048:NP * C + 3072], areaE[:, 1024:2048])]
        vB = areaD[0:B, :]
        Ft = areaE[:, 0:1024].rearrange("p (n j) -> p n j", n=NP)
        cI = areaE[:, 1024:1664].rearrange("p (k s j) -> p k s j", k=TERMS, s=2)
        Zl = areaE[0:D, 1664:2048].rearrange("p (l j) -> p l j", l=6)
        AT = sb("AT", [D, C])
        tp = sb("tp", [128, G, C])
        bc = tp[0:D, 0]
        scr = tp[0:D, 1]
        TAU = sb("TAU", [D, D])
        q_G, q_m, q_sg, q_se = (sb(n, [D, 1]) for n in ("q_G", "q_m", "q_sg", "q_se"))
        q_sq, q_nb, q_w, q_den = (sb(n, [D, 1]) for n in ("q_sq", "q_nb", "q_w", "q_den"))
        q_t1, q_cf = sb("q_t1", [D, 1]), sb("q_cf", [D, 1])
        tauc = sb("tauc", [D, 1])
        Vn = sb("Vn", [KC, NK, D])
        Z, Zt = sb("Z", [D, D]), sb("Zt", [D, D])
        Ztl = sb("Ztl", [D, 6, D])
        X, Xt = sb("X", [D, D]), sb("Xt", [D, D])
        P1, P2 = sb("P1", [D, D]), sb("P2", [D, D])
        tV = sb("tV", [D, D])
        Fq = sb("Fq", [D, 2, D])
        Us = sb("Us", [KC, NK, D])
        Ut = sb("Ut", [128, C])
        hT = sb("hT", [KC, NK, GT])
        xn = sb("xn", [128, G, C])
        st = sb("st", [128, G, 6])
        mv = sb("mv", [128, G, 2])
        ve = sb("ve", [128, G])
        held = sb("held", [1, 1])
        rs = sb("rs", [128, G])
        mx = sb("mx", [128, 32])
        rden = sb("rden", [128, 4, 4, 2])

        ident = cst[:, C_ID:C_ID + 128]
        i64 = cst[0:D, C_ID:C_ID + D]

        ld_c, ld_v, ld_ada, ld_q, ld_x, ld_xt = (sem(n) for n in ("ld_c", "ld_v", "ld_ada", "ld_q", "ld_x", "ld_xt"))
        ld_w, ld_m, ld_f = sem("ld_w"), sem("ld_m"), sem("ld_f")
        s_silu, s_exp = sem("s_silu"), sem("s_exp")
        s_vps, s_vsb, s_bounce = sem("s_vps"), sem("s_vsb"), sem("s_bounce")
        s_ada, s_adas, s_gps, s_gsb = sem("s_ada"), sem("s_adas"), sem("s_gps"), sem("s_gsb")
        s_gbc, s_gbs = sem("s_gbc"), sem("s_gbs")
        q_ch, q_sig, q_act = sem("q_ch"), sem("q_sig"), sem("q_act")
        s_b1, s_ft, s_mk, s_ci, e_h, e_sum = (sem(n) for n in ("s_b1", "s_ft", "s_mk", "s_ci", "e_h", "e_sum"))
        s_pe, s_dv = sem("s_pe"), sem("s_dv")
        s_am, e_pe, e_act = sem("s_am"), sem("e_pe"), sem("e_act")
        s_z, s_zs, s_w, s_ws, s_xr, s_xrs = (sem(n) for n in ("s_z", "s_zs", "s_w", "s_ws", "s_xr", "s_xrs"))
        dch = sem("dch")
        a_st, a_rs, a_xn, a_T, a_mod, a_hT = (sem(n) for n in ("a_st", "a_rs", "a_xn", "a_T", "a_mod", "a_hT"))
        a_Q, a_q, a_K, a_k, a_V, a_v = (sem(n) for n in ("a_Q", "a_q", "a_K", "a_k", "a_V", "a_v"))
        a_S, a_mx, a_sub, a_exp, a_PT, a_pt = (sem(n) for n in ("a_S", "a_mx", "a_sub", "a_exp", "a_PT", "a_pt"))
        a_PV, a_rd, a_o, a_OT, a_ot, a_Y, a_y, a_res = (sem(n) for n in (
            "a_PV", "a_rd", "a_o", "a_OT", "a_ot", "a_Y", "a_y", "a_res"))
        s_vz = sem("s_vz")
        m_st, m_rs, m_xn, m_T, m_mod, m_hT = (sem(n) for n in ("m_st", "m_rs", "m_xn", "m_T", "m_mod", "m_hT"))
        m_F, m_sq, m_hx, m_in, m_th, m_g = (sem(n) for n in ("m_F", "m_sq", "m_hx", "m_in", "m_th", "m_g"))
        m_Y, m_y, m_res, m_out = (sem(n) for n in ("m_Y", "m_y", "m_res", "m_out"))

        out_t = out.rearrange("(n t) c -> t n c", t=128)
        block = ctx.enter_context(nc.Block())

        @block.sync
        def _(sp):
            sp.dma_start(AT[:], PT_).then_inc(ld_q, 16)
            sp.dma_start(cst[:], consts).then_inc(ld_q, 16)
            sp.dma_start(cT[:], condT).then_inc(ld_c, 16)
            for h in range(2):
                sp.dma_start(wfold[:, :, 1024 * h:1024 * h + 1024], Wfold[:, :, 1024 * h:1024 * h + 1024]).then_inc(ld_v, 16)
            sp.dma_start(bfs, bfold).then_inc(ld_v, 16)
            sp.dma_start(wada, Wada).then_inc(ld_ada, 16)
            sp.dma_start(bac[:], bada_col).then_inc(ld_ada, 16)
            sp.dma_start(bag[:], bada_gate).then_inc(ld_ada, 16)
            sp.dma_start(xTs, xT).then_inc(ld_xt, 16)
            sp.dma_start(xs[:], x.rearrange("(n t) c -> t n c", t=128)).then_inc(ld_x, 16)
            sp.wait_ge(s_vsb, 4)
            sp.dma_start(scratch, vB).then_inc(s_bounce, 16)
            sp.wait_ge(s_bounce, 16)
            rows = scratch.rearrange("(n b) (r j) -> b r n j", b=2, j=D)
            for b in range(2):
                for half in range(2):
                    at = 64 * b + 32 * half
                    sp.dma_start(Fm[at:at + 32], rows[b]).then_inc(ld_f, 16)
            with sp.Fori(0, NG) as u:
                sp.wait_ge(m_res, 2 * u + 3)
                sp.dma_start(out_t[:, bass.ds(G * u, G)], xs[:, bass.ds(G * u, G)]).then_inc(m_out, 16)
            sp.wait_ge(m_out, 16 * NG)

        @block.gpsimd
        def _(pool):
            for t, src in ((wq, Wq), (wk, Wk), (wv, Wv), (wp, Wp), (bqs, bq), (bks, bk), (bvs, bv), (bps, bp)):
                pool.dma_start(t[:], src).then_inc(ld_w, 16)
            for t, src in ((wf1, Wf1), (wf2, Wf2), (bf1s, bf1), (bf2s, bf2)):
                pool.dma_start(t[:], src).then_inc(ld_m, 16)
            pool.wait_ge(ld_ada, 48)
            for a in (1, 3):
                pool.tensor_scalar(bac[:, a], bac[:, a], 1.0, None, ALU.add).then_inc(s_b1, 1)
            pool.wait_ge(ld_q, 32)
            pool.wait_ge(ld_f, 64)
            m1 = cst[:, C_M1:C_M1 + 32].unsqueeze(1).broadcast_to([128, NP, 32])
            m2 = cst[:, C_M2:C_M2 + 32].unsqueeze(1).broadcast_to([128, NP, 32])
            t1, t2 = XY[:, :, 0, 0:32], XY[:, :, 1, 0:32]
            pool.tensor_tensor(t1, Fm[:, :, 0:32], m1, ALU.mult).then_inc(s_mk, 1)
            pool.wait_ge(s_ft, 1)
            pool.tensor_tensor(t2, Ft[:, :, 0:32], m2, ALU.mult).then_inc(s_mk, 1)
            pool.wait_ge(s_mk, 2)
            for b in range(2):
                top, low = slice(64 * b, 64 * b + 32), slice(64 * b + 32, 64 * b + 64)
                pool.tensor_tensor(Am[top, :, 0:32], t1[top], t2[top], ALU.add).then_inc(s_am, 1)
                pool.wait_ge(s_am, 4 * b + 1)
                pool.tensor_copy(Am[top, :, 32:64], Fm[top, :, 32:64]).then_inc(s_am, 1)
                pool.wait_ge(s_am, 4 * b + 2)
                pool.tensor_scalar(Am[low, :, 0:32], Ft[low, :, 32:64], -1.0, None, ALU.mult).then_inc(s_am, 1)
                pool.wait_ge(s_am, 4 * b + 3)
                pool.tensor_tensor(Am[low, :, 32:64], t1[low], t2[low], ALU.add).then_inc(s_am, 1)
                pool.wait_ge(s_am, 4 * b + 4)
            for k in range(TERMS):
                for s in range(2):
                    coef = float((-1) ** k / factorial(2 * k + s))
                    pool.tensor_scalar(cI[:, k, s], cst[:, C_ID2:C_ID2 + D], coef, None, ALU.mult).then_inc(s_ci, 1)
            pool.wait_ge(s_ci, 2 * TERMS)
            for q in range(4):
                pool.wait_ge(e_act, 3 * q + 3)
                pool.tensor_tensor(XY[:, 4 * q:4 * q + 4], XY[:, 4 * q:4 * q + 4],
                                   cI[:, TERMS - 1].unsqueeze(1).broadcast_to([128, 4, 2, D]), ALU.add).then_inc(e_h, 1)
            for q in range(4):
                pool.wait_ge(e_act, E_ACT(E_STAGES - 1, q))
                pool.tensor_tensor(Bm[:, 4 * q:4 * q + 4], XY[:, 4 * q:4 * q + 4, 0], XY[:, 4 * q:4 * q + 4, 1],
                                   ALU.add).then_inc(e_sum, 1)

            def rstd(stat, done, n):
                pool.wait_ge(stat, n)
                pool.tensor_tensor(rs[:], ve[:], cst[:, C_HALF:C_HALF + G], ALU.pow).then_inc(done, 1)

            def shift(mod, done, n, which, g):
                pool.wait_ge(mod, n)
                pool.tensor_tensor(hT[:].rearrange("p k (b t) -> p k b t", b=4),
                                   hT[:].rearrange("p k (b t) -> p k b t", b=4),
                                   adaT[:, which, :, bass.ds(4 * g, 4)].unsqueeze(3).broadcast_to([KC, NK, 4, L]),
                                   ALU.add).then_inc(done, 1)

            def residual(yready, done, n, g, gate):
                pool.wait_ge(yready, n)
                pool.tensor_tensor(tp[:], tp[:], gate[:, bass.ds(G * g, G)], ALU.mult).then_inc(done, 1)
                pool.wait_ge(done, 2 * n)
                pool.tensor_tensor(xs[:, bass.ds(G * g, G)], xs[:, bass.ds(G * g, G)], tp[:], ALU.add).then_inc(done, 1)

            rstd(a_st, a_rs, 1)
            shift(a_mod, a_hT, 1, 0, 0)
            rstd(a_st, a_rs, 2)

            def step(g, prev, nxt, nxt2):
                if nxt:
                    shift(a_mod, a_hT, g + 2, 0, g + 1)
                if nxt2:
                    rstd(a_st, a_rs, g + 3)
                if prev:
                    residual(a_y, a_res, g, g - 1, gate_a)

            step(0, False, True, True)
            with pool.Fori(1, NG - 2) as g:
                step(g, True, True, True)
            step(NG - 2, True, True, False)
            step(NG - 1, True, False, False)
            residual(a_y, a_res, NG, NG - 1, gate_a)

            rstd(m_st, m_rs, 1)
            shift(m_mod, m_hT, 1, 2, 0)
            rstd(m_st, m_rs, 2)

            def mstep(u, prev, nxt, nxt2):
                if nxt:
                    shift(m_mod, m_hT, u + 2, 2, u + 1)
                if nxt2:
                    rstd(m_st, m_rs, u + 3)
                if prev:
                    residual(m_y, m_res, u, u - 1, gate_m)

            mstep(0, False, True, True)
            with pool.Fori(1, NG - 2) as u:
                mstep(u, True, True, True)
            mstep(NG - 2, True, True, False)
            mstep(NG - 1, True, False, False)
            residual(m_y, m_res, NG, NG - 1, gate_m)

        @block.scalar
        def _(act):
            act.wait_ge(ld_c, 16)
            nc.scalar.activation(eT[:], cT[:], ACT.Exp, scale=-1.0).then_inc(s_exp, 1)
            def skew_out(n):
                act.wait_ge(s_vps, n + 1)
                nc.scalar.activation(vB[:, 512 * n:512 * n + 512], ps[0:B, n, :], ACT.Copy,
                                     scale=1.0 / (1 << SQUARINGS)).then_inc(s_vsb, 1)

            def ada_out(a):
                if a == 0:
                    act.wait_ge(s_ada, 1)
                    act.wait_ge(s_b1, 2)
                for k in range(NK):
                    at = 32 * (NK * a + k)
                    nc.scalar.activation(adaT[:, a, k], ps[0:KC, 4, at:at + 32], ACT.Identity,
                                         bias=bac[:, a, k:k + 1]).then_inc(s_adas, 1)

            def gates_out():
                act.wait_ge(s_gps, 1)
                nc.scalar.activation(gates[:], ps[0:B, 5:7, 0:C], ACT.Copy).then_inc(s_gsb, 1)

            def gate_out(n):
                act.wait_ge(s_gbc, n + 1)
                nc.scalar.activation((gate_a if n < NP else gate_m)[:, n % NP], ps[:, 4 + n % 4, 0:C],
                                     ACT.Copy).then_inc(s_gbs, 1)

            def exp_out(stage, q):
                act.wait_ge(e_pe, 4 * stage + q + 1)
                src = ps[:, q, :].rearrange("p (n s j) -> p n s j", n=4, s=2)
                quarter = slice(4 * q, 4 * q + 4)
                if stage == 0:
                    src = ps[:, q, 0:4 * D].rearrange("p (n j) -> p n j", n=4)
                    nc.scalar.activation(Bm[:, quarter], src, ACT.Copy).then_inc(e_act, 1)
                    for s in range(2):
                        coef = float((-1) ** TERMS / factorial(2 * TERMS + s))
                        nc.scalar.activation(XY[:, quarter, s], src, ACT.Copy, scale=coef).then_inc(e_act, 1)
                elif stage == TERMS - 1:
                    nc.scalar.activation(XY[:, quarter], src, ACT.Copy, scale=2.0).then_inc(e_act, 1)
                elif stage == TERMS:
                    src = ps[:, q, 0:4 * D].rearrange("p (n j) -> p n j", n=4)
                    nc.scalar.activation(XY[:, quarter, 1], src, ACT.Copy, scale=-1.0).then_inc(e_act, 1)
                else:
                    nc.scalar.activation(XY[:, quarter], src, ACT.Copy).then_inc(e_act, 1)

            act.wait_ge(ld_q, 32)
            for j in range(D):
                act.wait_ge(q_sig, j + 1)
                rows = slice(0, D) if j < 32 else slice(32, D)
                nc.scalar.activation(q_sq[rows], q_sg[rows], ACT.Sqrt, scale=4.0).then_inc(q_act, 1)
                if 3 <= j < 7:
                    skew_out(j - 3)
                if 7 <= j < 9:
                    ada_out(2 * (j - 7))
                    ada_out(2 * (j - 7) + 1)
                if j == 8:
                    gates_out()
                for n in range(3 * (j - 9), min(3 * (j - 8), 2 * NP)):
                    if n >= 0:
                        gate_out(n)
                if j >= E_FIRST and j < E_FIRST + 4 * E_STAGES:
                    exp_out((j - E_FIRST) // 4, (j - E_FIRST) % 4)

            def k_out(n):
                act.wait_ge(a_K, n)
                for c in range(4):
                    src = ps[:, 4 + c // 2, 256 * (c % 2):256 * (c % 2) + 256].rearrange("p (e m) -> p e m", m=L)
                    for r in range(4):
                        at = slice(HR * r, HR * r + HR)
                        ins = nc.scalar.activation(kD[c][at, :, r], src[at], ACT.Identity, bias=bks[at, c:c + 1])
                    ins.then_inc(a_k, 1)

            def ot_out(n):
                act.wait_ge(a_OT, n)
                for g in range(G):
                    for q in range(2):
                        src = ps[0:72, 6 + g, :].rearrange("p (b q h t) -> p q h b t", b=2, q=2, h=2)[:, q]
                        nc.scalar.activation(oT[:, g, q].rearrange("p h (b t) -> p h b t", b=2), src,
                                             ACT.Copy).then_inc(a_ot, 1)

            def exps(n):
                for t in range(G):
                    act.wait_ge(a_sub, 4 * n - 2 + 2 * t)
                    nc.scalar.activation(Pm[:, t], Pm[:, t], ACT.Exp).then_inc(a_exp, 1)

            def pt_out(n):
                for i in range(4):
                    act.wait_ge(a_PT, 4 * n - 3 + i)
                    nc.scalar.activation(Pt[:, i // 2, i % 2].rearrange("p r m -> p (r m)"), ps[:, i, :],
                                         ACT.Copy).then_inc(a_pt, 1)

            act.wait_ge(ld_w, 16 * 8)
            act.wait_ge(s_vz, 7)
            k_out(1)

            def step(g, prev, nxt):
                if prev:
                    ot_out(g)
                exps(g + 1)
                if nxt:
                    k_out(g + 2)
                pt_out(g + 1)

            step(0, False, True)
            with act.Fori(1, NG - 1) as g:
                step(g, True, True)
            step(NG - 1, True, False)
            ot_out(NG)

            act.wait_ge(ld_m, 16 * 4)

            def mstep(u, prev):
                if prev:
                    act.wait_ge(m_g, u)
                for j in range(5):
                    act.wait_ge(m_F, 5 * u + j + 1)
                    for c in range(2 * j, min(2 * j + 2, NF)):
                        ins = nc.scalar.activation(hs[:, c], ps[:, j % 4, 256 * (c % 2):256 * (c % 2) + 256],
                                                   ACT.Square, bias=bf1s[:, c:c + 1])
                    ins.then_inc(m_sq, 1)
                act.wait_ge(m_in, 2 * u + 2)
                nc.scalar.activation(hs, hs, ACT.Tanh, scale=GELU_C).then_inc(m_th, 1)

            mstep(0, False)
            with act.Fori(1, NG) as u:
                mstep(u, True)

        @block.vector
        def _(dve):
            v = nc.vector
            count = [0]

            def link(ins):
                count[0] += 1
                ins.then_inc(dch, 1)
                dve.wait_ge(dch, count[0])

            dve.wait_ge(s_exp, 1)
            link(v.tensor_scalar(eT[:], eT[:], 1.0, None, ALU.add))
            link(v.reciprocal(eT[:], eT[:]))
            v.tensor_tensor(sT[:], eT[:], cT[:], ALU.mult).then_inc(s_silu, 1)
            steps = [0]

            def qr(ins):
                steps[0] += 1
                ins.then_inc(q_ch, 1)
                return steps[0]

            v.memset(TAU[:], 0.0).then_inc(q_ch, 1)
            steps[0] = 1
            dve.wait_ge(ld_q, 32)
            updated = 1
            for j in range(D):
                rows = slice(0, D) if j < 32 else slice(32, D)
                a, tail = AT[rows], bc[rows]
                dve.wait_ge(q_ch, updated)
                for at in ((0, 32) if j < 32 else (32,)):
                    src = slice(32 * (j // 32), 32 * (j // 32) + 32)
                    n = qr(v.stream_shuffle(bc[at:at + 32, j:C], AT[src, j:C], [j % 32] * 32))
                dve.wait_ge(q_ch, n)
                qr_sq = v.tensor_tensor_reduce(out=scr[rows, j:C], in0=tail[:, j:C], in1=tail[:, j:C], scale=1.0, scalar=0.0,
                                               op0=ALU.mult, op1=ALU.add, accum_out=q_sg[rows])
                qr_sq.then_inc(q_sig, 1)
                dve.wait_ge(q_sig, j + 1)
                dots = qr(v.tensor_tensor_reduce(out=scr[rows, j:C], in0=a[:, j:C], in1=tail[:, j:C], scale=1.0, scalar=0.0,
                                                 op0=ALU.mult, op1=ALU.add, accum_out=q_G[rows]))
                qr(v.tensor_scalar(q_se[rows], q_sg[rows], 1e-30, None, ALU.max))
                half = qr(v.tensor_scalar(q_m[rows], tail[:, j:j + 1], 0.0, -0.5, ALU.is_ge, ALU.add))
                dve.wait_ge(q_ch, half)
                dve.wait_ge(q_act, j + 1)
                n = qr(v.tensor_scalar(q_nb[rows], q_m[rows], q_sq[rows, 0:1], None, ALU.mult))
                dve.wait_ge(q_ch, n)
                n = qr(v.tensor_scalar(q_den[rows], tail[:, j:j + 1], q_nb[rows, 0:1], q_se[rows, 0:1], ALU.mult, ALU.add))
                w = qr(v.tensor_scalar(q_w[rows], a[:, j:j + 1], q_nb[rows, 0:1], q_G[rows, 0:1], ALU.mult, ALU.add))
                dve.wait_ge(q_ch, n)
                n = qr(v.reciprocal(TAU[rows, j:j + 1], q_den[rows]))
                t1 = qr(v.tensor_scalar(q_t1[rows], cst[rows, C_ID + j:C_ID + j + 1], q_nb[rows, 0:1], None, ALU.mult))
                dve.wait_ge(q_ch, n)
                n = qr(v.tensor_scalar(q_cf[rows], q_w[rows], TAU[rows, j:j + 1], cst[rows, C_NGT + j:C_NGT + j + 1],
                                       ALU.mult, ALU.mult))
                dve.wait_ge(q_ch, n)
                if j < D - 1:
                    updated = qr(v.scalar_tensor_tensor(out=a[:, j + 1:C], in0=tail[:, j + 1:C], scalar=q_cf[rows, 0:1],
                                                        in1=a[:, j + 1:C], op0=ALU.mult, op1=ALU.add))
                qr(v.tensor_scalar(a[:, j:j + 1], a[:, j:j + 1], cst[rows, C_LE + j:C_LE + j + 1], q_t1[rows, 0:1],
                                   ALU.mult, ALU.add))
                if j == FOLD_AT:
                    dve.wait_ge(ld_f, 64)
                    v.transpose(Ft.rearrange("p n j -> p (n j)"), Fm.rearrange("p n j -> p (n j)")).then_inc(s_ft, 1)
            dve.wait_ge(q_ch, steps[0])

            link(v.tensor_tensor_reduce(out=scr[:, 0:D], in0=TAU[:], in1=i64, scale=1.0, scalar=0.0, op0=ALU.mult,
                                        op1=ALU.add, accum_out=tauc[:]))
            dve.wait_ge(s_pe, 1)
            v.tensor_copy(Vn[:], ps[0:KC, 0, 0:NK * D].rearrange("p (k d) -> p k d", k=NK)).then_inc(s_dv, 1)
            link(v.tensor_scalar(tV[:], AT[:, 0:D], tauc[:, 0:1], None, ALU.mult))
            dve.wait_ge(s_pe, 2)
            link(v.tensor_scalar(Z[:], ps[0:D, 1, 0:D], tauc[:, 0:1], None, ALU.mult))
            link(v.tensor_tensor(Z[:], Z[:], cst[0:D, C_UP:C_UP + D], ALU.mult))
            v.tensor_tensor(Zl[:], Z[:].unsqueeze(1).broadcast_to([D, 6, D]),
                            cst[0:D, C_LV:C_LV + 384].rearrange("p (l j) -> p l j", l=6), ALU.mult).then_inc(s_dv, 1)
            dve.wait_ge(s_pe, 3)
            v.tensor_copy(Ztl[:], ps[0:D, 2, 0:384].rearrange("p (l j) -> p l j", l=6)).then_inc(s_dv, 1)
            v.tensor_tensor(X[:], i64, Zl[:, 0], ALU.subtract).then_inc(s_dv, 1)
            dve.wait_ge(s_dv, 3)
            v.tensor_tensor(Xt[:], i64, Ztl[:, 0], ALU.subtract).then_inc(s_dv, 1)
            for level in range(1, 6):
                dve.wait_ge(s_pe, 3 + 2 * level - 1)
                v.tensor_copy(P1[:], ps[0:D, 0, 0:D]).then_inc(s_dv, 1)
                v.tensor_copy(P2[:], ps[0:D, 0, D:2 * D]).then_inc(s_dv, 1)
                dve.wait_ge(s_pe, 3 + 2 * level)
                v.tensor_tensor(X[:], X[:], ps[0:D, 1, 0:D], ALU.subtract).then_inc(s_dv, 1)
                v.tensor_tensor(Xt[:], Xt[:], ps[0:D, 1, D:2 * D], ALU.subtract).then_inc(s_dv, 1)
            dve.wait_ge(s_pe, 14)
            v.tensor_copy(Fq[:, 0], ps[0:D, 2, 0:D]).then_inc(s_dv, 1)
            v.tensor_copy(Fq[:, 1], ps[0:D, 2, 0:D]).then_inc(s_dv, 1)
            dve.wait_ge(s_pe, 15)
            v.tensor_tensor(Us[:, 0], cst[0:KC, C_ID:C_ID + D], ps[0:KC, 3, 0:D], ALU.subtract).then_inc(s_dv, 1)
            v.tensor_scalar(Us[:, 1:3], ps[0:KC, 3, D:3 * D].rearrange("p (k d) -> p k d", k=2), -1.0, None,
                            ALU.mult).then_inc(s_dv, 1)
            v.tensor_scalar(Ut[:], ps[:, 4, 0:C], -1.0, None, ALU.mult).then_inc(s_dv, 1)
            dve.wait_ge(s_dv, 30)
            v.tensor_tensor(Ut[:, 0:D], Ut[:, 0:D], cst[:, C_ID2:C_ID2 + D], ALU.add).then_inc(s_dv, 1)

            for h in range(2):
                dve.wait_ge(s_z, h + 1)
                v.tensor_copy(zT[:, 8 * h:8 * h + 8], ps[:, 4 + h, :].rearrange("p (n t) -> p n t", n=8)).then_inc(s_zs, 1)
            for h in range(2):
                dve.wait_ge(s_w, h + 1)
                v.tensor_scalar(wT[:, 8 * h:8 * h + 8], ps[:, 6 + h, :].rearrange("p (n t) -> p n t", n=8),
                                0.5, None, ALU.mult).then_inc(s_ws, 1)
            dve.wait_ge(ld_x, 16)
            for n in range(NP):
                dve.wait_ge(s_xr, n + 1)
                v.tensor_tensor(xs[:, n], xs[:, n], ps[:, n % 4, 0:C], ALU.add).then_inc(s_xrs, 1)

            v.memset(areaD[:, 0:G * 8 * 4 * VW], 0.0).then_inc(s_vz, 1)
            dve.wait_ge(s_vz, 1)
            for b in range(2):
                v.memset(Vb[64 * b:64 * b + 64, :, :, b].rearrange("p g n (h v) -> p (g n) h v", v=VW)[:, :, :, DH], 1.0
                         ).then_inc(s_vz, 1)
            for c in range(4):
                v.memset(kD[c], 0.0).then_inc(s_vz, 1)
            dve.wait_ge(ld_w, 16 * 8)
            dve.wait_ge(s_xrs, NP)

            def stats(stat, rstd, xnd, n, g):
                for t in range(G):
                    v.bn_stats(st[:, t], xs[:, bass.ds(G * g + t, 1)].rearrange("p a c -> p (a c)")).then_inc(stat[1], 1)
                dve.wait_ge(stat[1], 5 * n - 3)
                v.memset(held[:], 0.0).then_inc(stat[1], 1)
                for t in range(G):
                    v.bn_aggr(mv[:, t], st[:, t]).then_inc(stat[1], 1)
                dve.wait_ge(stat[1], 5 * n)
                v.tensor_scalar(ve[:], mv[:, :, 1], LN_EPS, None, ALU.add).then_inc(stat[0], 1)
                dve.wait_ge(rstd, n)
                for t in range(G):
                    v.tensor_scalar(xn[:, t], xs[:, bass.ds(G * g + t, 1)].rearrange("p a c -> p (a c)"),
                                    mv[:, t, 0:1], rs[:, t:t + 1], ALU.subtract, ALU.mult).then_inc(xnd, 1)

            def scale(T, mod, n, which, g):
                dve.wait_ge(T, n)
                src = ps[0:KC, 4:6, :].rearrange("p b n -> p (b n)")[:, 0:NK * GT].rearrange(
                    "p (k b t) -> p k b t", k=NK, b=4)
                v.tensor_tensor(hT[:].rearrange("p k (b t) -> p k b t", b=4), src,
                                adaT[:, which, :, bass.ds(4 * g, 4)].unsqueeze(3).broadcast_to([KC, NK, 4, L]),
                                ALU.mult).then_inc(mod, 1)

            def q_out(n):
                dve.wait_ge(a_Q, n)
                for c in range(4):
                    v.tensor_scalar(qT[:, c], ps[:, 6 + c // 2, 256 * (c % 2):256 * (c % 2) + 256], bqs[:, c:c + 1],
                                    float(DH) ** -0.5, ALU.add, ALU.mult).then_inc(a_q, 1)

            def v_out(n):
                dve.wait_ge(a_V, n)
                for g in range(G):
                    for b in range(2):
                        at = slice(64 * b, 64 * b + 64)
                        v.tensor_tensor(
                            Vb[at, g, :, b].rearrange("p n (h v) -> p n h v", v=VW)[:, :, :, 0:DH],
                            ps[at, 6 + g, 0:C].rearrange("p (n h d) -> p n h d", n=8, h=2),
                            bvs[at, :].rearrange("p (n h d) -> p n h d", n=8, h=2), ALU.add).then_inc(a_v, 1)

            def maxima(n):
                dve.wait_ge(a_S, n)
                v.tensor_reduce(mx[:].rearrange("p (e r) -> p e r", e=4), ps[:, 0:4, :].rearrange("p e (r m) -> p e r m", m=L),
                                AX.X, ALU.max).then_inc(a_mx, 1)
                dve.wait_ge(a_mx, n)
                for e in range(4):
                    v.tensor_tensor(Pm[:, e // 2].rearrange("p q r b m -> p (q r) b m")[:, :, e % 2],
                                    ps[:, e, :].rearrange("p (r m) -> p r m", m=L),
                                    mx[:, 8 * e:8 * e + 8].unsqueeze(2).broadcast_to([128, 8, L]),
                                    ALU.subtract).then_inc(a_sub, 1)

            def norm(n):
                for g in range(G):
                    dve.wait_ge(a_PV, 2 * n - 1 + g)
                    for h in range(2):
                        at = slice(64 * h, 64 * h + 64)
                        src = ps[at, 4 + 2 * g:6 + 2 * g, 0:304].rearrange("p q (r b v) -> p q r b v", r=4, b=2)
                        v.reciprocal(rden[at, 2 * g:2 * g + 2], src[:, :, :, :, h * VW + DH]).then_inc(a_rd, 1)
                    dve.wait_ge(a_rd, 4 * n - 2 + 2 * g)
                    for h in range(2):
                        at = slice(64 * h, 64 * h + 64)
                        for q in range(2):
                            src = ps[at, 4 + 2 * g + q, 0:304].rearrange("p (r b v) -> p r b v", r=4, b=2)
                            v.tensor_tensor(
                                oN[at, g, :, 4 * q:4 * q + 4].rearrange("p b r d -> p r b d"),
                                src[:, :, :, h * VW:h * VW + DH],
                                rden[at, 2 * g + q].unsqueeze(3).broadcast_to([64, 4, 2, DH]),
                                ALU.mult).then_inc(a_o, 1)

            def proj_out(Y, y, res, n, bank, bias, half):
                dve.wait_ge(res, 2 * n - 1)
                dve.wait_ge(Y, G * n)
                if half is None:
                    v.tensor_tensor(tp[:], ps[:, bank:bank + 2, 0:C], bias[:].unsqueeze(1).broadcast_to([128, G, C]),
                                    ALU.add).then_inc(y, 1)
                else:
                    v.scalar_tensor_tensor(out=tp[:], in0=ps[:, bank:bank + 2, 0:C], scalar=half,
                                           in1=bias[:].unsqueeze(1).broadcast_to([128, G, C]),
                                           op0=ALU.mult, op1=ALU.add).then_inc(y, 1)

            v.memset(tp[:, 0, 0:1], 0.0).then_inc(a_res, 1)
            v.memset(tp[:, 1, 0:1], 0.0).then_inc(m_res, 1)
            A_ST = (a_st, dch2 := sem("a_bn"))
            stats(A_ST, a_rs, a_xn, 1, 0)
            scale(a_T, a_mod, 1, 1, 0)
            stats(A_ST, a_rs, a_xn, 2, 1)
            q_out(1)
            v_out(1)

            def step(g, prev, nxt, nxt2):
                if nxt:
                    dve.wait_ge(a_V, g + 1)
                    scale(a_T, a_mod, g + 2, 1, g + 1)
                if nxt2:
                    stats(A_ST, a_rs, a_xn, g + 3, g + 2)
                maxima(g + 1)
                if prev:
                    proj_out(a_Y, a_y, a_res, g, 6, bps, None)
                if nxt:
                    q_out(g + 2)
                norm(g + 1)
                if nxt:
                    v_out(g + 2)

            step(0, False, True, True)
            with dve.Fori(1, NG - 2) as g:
                step(g, True, True, True)
            step(NG - 2, True, True, False)
            step(NG - 1, True, False, False)
            proj_out(a_Y, a_y, a_res, NG, 6, bps, None)

            dve.wait_ge(a_res, 2 * NG + 1)
            dve.wait_ge(ld_m, 16 * 4)
            M_ST = (m_st, sem("m_bn"))
            stats(M_ST, m_rs, m_xn, 1, 0)
            scale(m_T, m_mod, 1, 3, 0)
            stats(M_ST, m_rs, m_xn, 2, 1)

            def mstep(u, prev, nxt, nxt2):
                for j in range(5):
                    dve.wait_ge(m_sq, 5 * u + j + 1)
                    for c in range(2 * j, min(2 * j + 2, NF)):
                        ins = v.tensor_scalar(hx[:, c], ps[:, j % 4, 256 * (c % 2):256 * (c % 2) + 256],
                                              bf1s[:, c:c + 1], None, ALU.add)
                        ins.then_inc(m_hx, 1)
                if nxt:
                    scale(m_T, m_mod, u + 2, 3, u + 1)
                v.tensor_scalar(hs[:], hs[:], GELU_A, 1.0, ALU.mult, ALU.add).then_inc(m_in, 1)
                dve.wait_ge(m_in, 2 * u + 1)
                dve.wait_ge(m_hx, 9 * u + 9)
                v.tensor_tensor(hs[:], hs[:], hx[:], ALU.mult).then_inc(m_in, 1)
                if nxt2:
                    stats(M_ST, m_rs, m_xn, u + 3, u + 2)
                if prev:
                    proj_out(m_Y, m_y, m_res, u, 6, bf2s, 0.5)
                dve.wait_ge(m_th, u + 1)
                v.scalar_tensor_tensor(out=hg[:], in0=hs[:], scalar=1.0, in1=hx[:], op0=ALU.add,
                                       op1=ALU.mult).then_inc(m_g, 1)

            mstep(0, False, True, True)
            with dve.Fori(1, NG - 2) as u:
                mstep(u, True, True, True)
            mstep(NG - 2, True, True, False)
            mstep(NG - 1, True, False, False)
            proj_out(m_Y, m_y, m_res, NG, 6, bf2s, 0.5)

        @block.tensor
        def _(pe):
            def mm(out_, lhsT, rhs, first=True, last=True):
                return nc.tensor.matmul(out_, lhsT, rhs, start=first, stop=last)

            ones = cst[0:1, C_ONES:C_ONES + B]
            pe.wait_ge(ld_q, 32)
            pe.wait_ge(s_silu, 1)
            pe.wait_ge(ld_v, 48)
            for n in range(4):
                for k in range(NK):
                    mm(ps[0:B, n, :], sT[:, k], wfold[:, k, 512 * n:512 * n + 512], k == 0, False)
                mm(ps[0:B, n, :], ones, bfs[:, 512 * n:512 * n + 512], False, True).then_inc(s_vps, 1)
            pe.wait_ge(ld_ada, 48)
            for a, part in enumerate((0, 1, 3, 4)):
                for c in range(NK):
                    for k in range(NK):
                        col = part * C + c * KC
                        ins = mm(ps[0:KC, 4, 32 * (NK * a + c):32 * (NK * a + c) + 32], wada[:, k, col:col + KC],
                                 sT[:, k], k == 0, k == NK - 1)
            ins.then_inc(s_ada, 1)
            for n, part in enumerate((2, 5)):
                for k in range(NK):
                    mm(ps[0:B, 5 + n, 0:C], sT[:, k], wada[:, k, part * C:part * C + C], k == 0, False)
                ins = mm(ps[0:B, 5 + n, 0:C], ones, bag[:, n], False, True)
            ins.then_inc(s_gps, 1)
            pe.wait_ge(s_gsb, 1)
            pe.wait_ge(s_adas, 4 * NK)
            for n in range(2 * NP):
                if n >= 4:
                    pe.wait_ge(s_gbs, n - 3)
                p = n % NP
                for b in range(2):
                    one = cst[0:B, C_ID + 2 * p + b:C_ID + 2 * p + b + 1].broadcast_to([B, L])
                    ins = mm(ps[64 * b:64 * b + 64, 4 + n % 4, 0:C], one, gates[:, n // NP])
                ins.then_inc(s_gbc, 1)

            def product(left, right, width, q, added):
                for lhs, rhs, out_ in added:
                    nc.tensor.matmul(out_, lhs, rhs, start=rhs is added[0][1], stop=False, skip_group_check=True)
                for n in range(4):
                    for b in range(2):
                        at = slice(64 * b, 64 * b + 64)
                        ins = nc.tensor.matmul(ps[at, q, width * n:width * n + width], left[at, 4 * q + n],
                                               right[at, 4 * q + n], start=not added and n == 0, stop=True,
                                               skip_group_check=True)
                ins.then_inc(e_pe, 1)

            pe.wait_ge(s_am, 8)
            pe.wait_ge(s_vsb, 4)
            for stage in range(E_STAGES):
                for q in range(4):
                    bank = ps[:, q, :].rearrange("p (n s j) -> p n s j", n=4, s=2)
                    mine = slice(4 * q, 4 * q + 4)
                    if stage == 0:
                        product(Am, Am, D, q, [])
                        continue
                    if stage == 1:
                        pe.wait_ge(e_h, q + 1)
                    else:
                        pe.wait_ge(e_act, E_ACT(stage - 1, q))
                    if stage < TERMS:
                        k = TERMS - 1 - stage
                        added = [] if k == 0 else [
                            (ident, cI[:, k].unsqueeze(1).broadcast_to([128, 4, 2, D]), bank)]
                        product(Bm, XY, 2 * D, q, added)
                    elif stage == TERMS:
                        product(Am, XY[:, :, 1], D, q,
                                [(cst[:, C_N2I:C_N2I + 128], Am[:, mine], ps[:, q, 0:4 * D].rearrange("p (n j) -> p n j", n=4))])
                    else:
                        product(XY[:, :, 0], XY, 2 * D, q,
                                [(cst[:, C_4I:C_4I + 128], XY[:, mine, 0], bank[:, :, 0]),
                                 (cst[:, C_2I:C_2I + 128], XY[:, mine, 1], bank[:, :, 1])])

            pe.wait_ge(q_ch, QR_STEPS)
            pe.wait_ge(s_gbs, 2 * NP)
            pe.wait_ge(e_act, E_ACT(E_STAGES - 1, 3))
            for k in range(NK):
                ins = nc.tensor.transpose(ps[0:KC, 0, D * k:D * k + D], AT[:, KC * k:KC * k + KC], i64)
            ins.then_inc(s_pe, 1)
            pe.wait_ge(s_dv, 1)
            for k in range(NK):
                ins = mm(ps[0:D, 1, 0:D], Vn[:, k], Vn[:, k], k == 0, k == NK - 1)
            ins.then_inc(s_pe, 1)
            pe.wait_ge(s_dv, 2)
            for level in range(6):
                ins = nc.tensor.transpose(ps[0:D, 2, D * level:D * level + D], Zl[:, level], i64)
            ins.then_inc(s_pe, 1)
            for level in range(1, 6):
                pe.wait_ge(s_dv, 5 + 4 * (level - 1))
                mm(ps[0:D, 0, 0:D], Ztl[:, level], X[:])
                mm(ps[0:D, 0, D:2 * D], Zl[:, level], Xt[:]).then_inc(s_pe, 1)
                pe.wait_ge(s_dv, 5 + 4 * (level - 1) + 2)
                mm(ps[0:D, 1, 0:D], Xt[:], P1[:])
                mm(ps[0:D, 1, D:2 * D], X[:], P2[:]).then_inc(s_pe, 1)
            pe.wait_ge(s_dv, 25)
            mm(ps[0:D, 2, 0:D], Xt[:], tV[:]).then_inc(s_pe, 1)
            pe.wait_ge(s_dv, 27)
            for k in range(NK):
                mm(ps[0:KC, 3, D * k:D * k + D], AT[:, KC * k:KC * k + KC], Fq[:, 0])
            mm(ps[:, 4, 0:C], Fq[:].rearrange("p a b -> p (a b)"), AT[:]).then_inc(s_pe, 1)

            pe.wait_ge(s_dv, 31)
            pe.wait_ge(ld_xt, 16)
            for h in range(2):
                for k in range(NK):
                    for b in range(2):
                        rhs = xTs[:, k].rearrange("p (n b t) -> p b n t", b=2, t=L)[:, b, 8 * h:8 * h + 8]
                        ins = mm(ps[64 * b:64 * b + 64, 4 + h, :], Us[:, k], rhs, k == 0, k == NK - 1)
                ins.then_inc(s_z, 1)
            pe.wait_ge(e_sum, 4)
            for h in range(2):
                pe.wait_ge(s_zs, h + 1)
                for n in range(8 * h, 8 * h + 8):
                    for b in range(2):
                        at = slice(64 * b, 64 * b + 64)
                        ins = mm(ps[at, 6 + h, L * (n % 8):L * (n % 8) + L], Bm[at, n], zT[at, n])
                ins.then_inc(s_w, 1)
            for n in range(NP):
                pe.wait_ge(s_ws, n // 8 + 1)
                if n >= 4:
                    pe.wait_ge(s_xrs, n - 3)
                for b in range(2):
                    at = slice(64 * b, 64 * b + 64)
                    ins = mm(ps[at, n % 4, 0:C], wT[at, n], Ut[at])
                ins.then_inc(s_xr, 1)

            def turn(xnd, T, n):
                pe.wait_ge(xnd, G * n)
                flat = ps[0:KC, 4:6, :].rearrange("p b n -> p (b n)")
                for k in range(NK):
                    for t in range(G):
                        ins = nc.tensor.transpose(flat[:, GT * k + 128 * t:GT * k + 128 * t + 128],
                                                  xn[:, t, KC * k:KC * k + KC], ident)
                ins.then_inc(T, 1)

            def qk(w, bank, ready, n):
                for c in range(4):
                    for k in range(NK):
                        ins = mm(ps[:, bank + c // 2, 256 * (c % 2):256 * (c % 2) + 256],
                                 w[:, k, 128 * c:128 * c + 128], hT[:, k], k == 0, k == NK - 1)
                ins.then_inc(ready, 1)

            def values(n):
                for t in range(G):
                    for k in range(NK):
                        ins = mm(ps[:, 6 + t, 0:C], hT[:, k, 128 * t:128 * t + 128], wv[:, k], k == 0, k == NK - 1)
                ins.then_inc(a_V, 1)

            def scores(n):
                pe.wait_ge(a_q, 4 * n)
                pe.wait_ge(a_k, 4 * n)
                for e in range(2 * G):
                    for q in range(2):
                        for h in range(2):
                            ins = mm(ps[64 * h:64 * h + 64, e, 256 * q:256 * q + 256],
                                     qT[:, 2 * q + h, L * e:L * e + L], kD[2 * q + h][:, e].rearrange("p r m -> p (r m)"))
                ins.then_inc(a_S, 1)

            def turn_out(n):
                pe.wait_ge(a_o, 8 * n)
                for g in range(G):
                    for b in range(2):
                        for q in range(2):
                            ins = nc.tensor.transpose(ps[0:72, 6 + g, 256 * b + 128 * q:256 * b + 128 * q + 128],
                                                      oN[:, g, b, 4 * q:4 * q + 4].rearrange("p r d -> p (r d)"), ident)
                ins.then_inc(a_OT, 1)

            def project(n):
                pe.wait_ge(a_ot, 4 * n)
                for t in range(G):
                    for c in range(4):
                        ins = mm(ps[:, 6 + t, 0:C], oT[:, t, c // 2, c % 2], wp[:, c], c == 0, c == 3)
                    ins.then_inc(a_Y, 1)

            def turn_p(n):
                for t in range(G):
                    pe.wait_ge(a_exp, 2 * n - 1 + t)
                    for q in range(2):
                        for r in range(4):
                            ins = nc.tensor.transpose(ps[:, 2 * t + q, 128 * r:128 * r + 128],
                                                      Pm[:, t, q, r].rearrange("p b m -> p (b m)"), ident)
                        ins.then_inc(a_PT, 1)

            def pv(n, g):
                pe.wait_ge(a_pt, 4 * n - 2 + 2 * g)
                if g == 0:
                    pe.wait_ge(a_v, 4 * n)
                for q in range(2):
                    for r in range(4):
                        ins = mm(ps[:, 4 + 2 * g + q, 4 * VW * r:4 * VW * r + 4 * VW], Pt[:, g, q, r],
                                 Vb[:, g, 4 * q + r].rearrange("p b v -> p (b v)"))
                ins.then_inc(a_PV, 1)

            pe.wait_ge(s_vz, 3)
            pe.wait_ge(ld_w, 16 * 8)
            turn(a_xn, a_T, 1)
            pe.wait_ge(a_hT, 1)
            qk(wk, 4, a_K, 1)
            qk(wq, 6, a_Q, 1)
            pe.wait_ge(a_k, 4)
            turn(a_xn, a_T, 2)
            pe.wait_ge(a_q, 4)
            values(1)

            def step(g, prev, nxt, nxt2):
                scores(g + 1)
                if prev:
                    pe.wait_ge(a_v, 4 * (g + 1))
                    turn_out(g)
                if nxt:
                    pe.wait_ge(a_hT, g + 2)
                    qk(wk, 4, a_K, g + 2)
                if prev:
                    project(g)
                turn_p(g + 1)
                if prev:
                    pe.wait_ge(a_y, g)
                if nxt:
                    qk(wq, 6, a_Q, g + 2)
                    pe.wait_ge(a_k, 4 * (g + 2))
                pv(g + 1, 0)
                if nxt:
                    pe.wait_ge(a_q, 4 * (g + 2))
                pv(g + 1, 1)
                if nxt2:
                    pe.wait_ge(a_o, 8 * g + 4)
                    turn(a_xn, a_T, g + 3)
                if nxt:
                    pe.wait_ge(a_o, 8 * g + 8)
                    values(g + 2)
                    
            step(0, False, True, True)
            with pe.Fori(1, NG - 2) as g:
                step(g, True, True, True)
            step(NG - 2, True, True, False)
            step(NG - 1, True, False, False)
            turn_out(NG)
            project(NG)

            def hidden(u):
                pe.wait_ge(m_hT, u + 1)
                for j in range(5):
                    if j == 4:
                        pe.wait_ge(m_hx, 9 * u + 2)
                    for c in range(2 * j, min(2 * j + 2, NF)):
                        for k in range(NK):
                            ins = mm(ps[:, j % 4, 256 * (c % 2):256 * (c % 2) + 256],
                                     wf1[:, k, 128 * c:128 * c + 128], hT[:, k], k == 0, k == NK - 1)
                    ins.then_inc(m_F, 1)

            def down(n):
                pe.wait_ge(m_g, n)
                for t in range(G):
                    for c in range(NF):
                        ins = mm(ps[:, 6 + t, 0:C], hg[:, c, 128 * t:128 * t + 128], wf2[:, c], c == 0, c == NF - 1)
                    ins.then_inc(m_Y, 1)

            pe.wait_ge(ld_m, 16 * 4)
            pe.wait_ge(a_y, NG)
            turn(m_xn, m_T, 1)

            def mstep(u, prev, nxt):
                if prev:
                    pe.wait_ge(m_hx, 9 * u)
                hidden(u)
                if nxt:
                    turn(m_xn, m_T, u + 2)
                if prev:
                    down(u)

            mstep(0, False, True)
            with pe.Fori(1, NG - 1) as u:
                mstep(u, True, True)
            mstep(NG - 1, True, False)
            down(NG)


def kernel(x, cond_1152, L0_cond_P, L0_cond_W, L0_cond_b, L1_cond_W_qkv, L1_cond_b_qkv, L1_cond_W_proj,
           L1_cond_b_proj, L1_cond_W_fc1, L1_cond_b_fc1, L1_cond_W_fc2, L1_cond_b_fc2, L1_cond_W_ada, L1_cond_b_ada):
    import concourse.bacc as bacc
    from concourse.bass_utils import run_bass_kernel_spmd

    def chunks(a):
        return a.reshape(NK, KC, -1).transpose(1, 0, 2)

    def rep(a, n):
        return np.tile(np.asarray(a)[None], (n,) + (1,) * np.asarray(a).ndim)

    def heads(a):
        a = a.reshape(-1, 2, 4, 2, DH).transpose(0, 1, 3, 2, 4)
        padded = np.zeros(a.shape[:-1] + (HR,), np.float32)
        padded[..., :DH] = a
        return padded.reshape(padded.shape[0], 512)

    tokens = np.asarray(x).reshape(B * L, C)
    Wr, br = np.asarray(L0_cond_W), np.asarray(L0_cond_b)
    packed = np.zeros((D, D), np.int64)
    packed[np.triu_indices(D, 1)] = np.arange(D * (D - 1) // 2)
    fold_w = np.zeros((32, D, C), np.float32)
    fold_b = np.zeros((32, D), np.float32)
    for r in range(32):
        for c in range(D):
            if c != r:
                k = packed[r, c] if c > r else packed[32 + c, 32 + r]
                fold_w[r, c], fold_b[r, c] = Wr[k], br[k]
    Wqkv, bqkv = np.asarray(L1_cond_W_qkv), np.asarray(L1_cond_b_qkv)
    bada = np.asarray(L1_cond_b_ada).reshape(6, C)
    arrays = {
        "x": tokens,
        "xT": chunks(tokens.T),
        "condT": chunks(np.asarray(cond_1152).T),
        "PT": np.asarray(L0_cond_P).T,
        "Wfold": chunks(fold_w.reshape(2048, C).T),
        "bfold": fold_b.reshape(1, 2048),
        "Wada": chunks(np.asarray(L1_cond_W_ada)),
        "bada_col": bada[[0, 1, 3, 4]].reshape(4, NK, KC).transpose(2, 0, 1),
        "bada_gate": bada[[2, 5]][None],
        "Wq": chunks(heads(Wqkv[:, 0:C])),
        "Wk": chunks(heads(Wqkv[:, C:2 * C])),
        "bq": heads(bqkv[None, 0:C]).reshape(4, 128).T,
        "bk": heads(bqkv[None, C:2 * C]).reshape(4, 128).T,
        "Wv": chunks(Wqkv[:, 2 * C:]),
        "bv": rep(bqkv[2 * C:], 128),
        "Wp": np.asarray(L1_cond_W_proj).reshape(2, 4, 2, DH, C).transpose(1, 3, 0, 2, 4).reshape(72, 4, C),
        "bp": rep(L1_cond_b_proj, 128),
        "Wf1": chunks(np.asarray(L1_cond_W_fc1)),
        "bf1": np.asarray(L1_cond_b_fc1).reshape(NF, 128).T,
        "Wf2": np.asarray(L1_cond_W_fc2).reshape(NF, 128, C).transpose(1, 0, 2),
        "bf2": rep(L1_cond_b_fc2, 128),
        "consts": constants(),
    }
    nc = bacc.Bacc("TRN2", target_bir_lowering=False, num_devices=1)
    feed, args = {}, []
    for name, a in arrays.items():
        a = np.ascontiguousarray(a)
        feed[f"in_{name}"] = a
        args.append(nc.dram_tensor(f"in_{name}", a.shape, F32, kind="ExternalInput").ap())
    args.append(nc.dram_tensor("skew_scratch", (B, 2048), F32, kind="Internal").ap())
    args.append(nc.dram_tensor("out", (B * L, C), F32, kind="ExternalOutput").ap())
    cond_block_kernel(nc, *args)
    r = run_bass_kernel_spmd(nc, [feed], core_ids=[0])
    return r.results[0]["out"].reshape(B, L, C)
```

```python
from contextlib import ExitStack
from math import factorial

import numpy as np
import concourse.bass as bass
from concourse import mybir

ALU = mybir.AluOpType
ACT = mybir.ActivationFunctionType
AX = mybir.AxisListType
F32 = mybir.dt.float32

B, L, C = 32, 64, 288
H, DH = 16, 18
D = 64
FF = 4 * C
KC, NK = 96, C // 96
NP = B // 2
G = 2
NG = NP // G
GT = G * 128
NF = FF // 128
HEADS = ((0, 6), (6, 11), (11, 16))
WHOLE, PAIRS = (slice(0, GT),), (slice(0, 128), slice(128, GT))
HP = 6 * DH
PIECES = ((0, 0, 6), (1, 6, 8), (1, 8, 11), (2, 11, 16))
VW = DH + 1
SQUARINGS = 9
TERMS = 5
LN_EPS = 1e-6
GELU_C = float(np.sqrt(2.0 / np.pi))
GELU_A = 0.044715

C_ID = 0
C_ID2 = 128
C_M1 = C_ID2 + 64
C_M2 = C_M1 + 32
C_NGT = C_M2 + 32
C_LE = C_NGT + 64
C_LV = C_LE + 64
C_LVT = C_LV + 6 * 64
C_HALF = C_LVT + 6 * 64
C_4I = C_HALF + 2
C_2I = C_4I + 128
C_N2I = C_2I + 128
C_ONES = C_N2I + 128
C_HM = C_ONES + B
NCONST = C_HM + 6


E_STAGES = 1 + (TERMS - 1) + 1 + SQUARINGS
E_FIRST = 16
E_OUTS = [4] + (TERMS - 2) * [1] + [3, 1] + (SQUARINGS - 1) * [3] + [1]
SKEW_AT = 5
ADA_AT = 11
FOLD_AT = 9


def E_BEFORE(j):
    return max(0, j - E_FIRST) * 4 * E_STAGES // (D - E_FIRST)


def E_ACT(stage, q):
    return 4 * sum(E_OUTS[:stage]) + (q + 1) * E_OUTS[stage]


def constants():
    c = np.zeros((128, NCONST), np.float32)
    i = np.arange(128)
    c[i, C_ID + i] = 1
    c[i, C_ID2 + i % 64] = 1
    r, q = np.arange(32)[:, None], np.arange(32)[None, :]
    for p in range(4):
        top = p % 2 == 0
        c[32 * p:32 * p + 32, C_M1:C_M1 + 32] = (q > r) if top else -1.0 * (q < r)
        c[32 * p:32 * p + 32, C_M2:C_M2 + 32] = -1.0 * (q < r) if top else (q > r)
    i, j = np.arange(64)[:, None], np.arange(64)[None, :]
    c[:64, C_NGT:C_NGT + 64] = -1.0 * (i > j)
    c[:64, C_LE:C_LE + 64] = i <= j
    for level in range(6):
        s = 1 << level
        c[:64, C_LV + 64 * level:C_LV + 64 * level + 64] = ((i // s) % 2 == 0) & (j // s == i // s + 1)
        c[:64, C_LVT + 64 * level:C_LVT + 64 * level + 64] = ((j // s) % 2 == 0) & (i // s == j // s + 1)
    c[:, C_HALF:C_HALF + 2] = -0.5
    for at, value in ((C_4I, 4), (C_2I, 2), (C_N2I, -2)):
        c[np.arange(128), at + np.arange(128)] = value
    c[:, C_ONES:C_HM] = 1
    for head in range(6):
        c[DH * head:DH * head + DH, C_HM + head] = 1
    return c


def cond_block_kernel(nc, x, xT, condT, PT_, Wfold, bfold, Wada, bada_col, bada_gate, Wq, Wk, bq, bk,
                      Wv, bv, Wp, bp, Wf1, bf1, Wf2, bf2, consts, scratch, gate_scratch, out):
    with ExitStack() as ctx:
        def sb(name, shape):
            return ctx.enter_context(nc.sbuf_tensor(name, shape, F32))

        def sem(name):
            return ctx.enter_context(nc.semaphore(name))

        ps = ctx.enter_context(nc.psum_tensor("ps", [128, 8, 512], F32))

        cst = sb("cst", [128, NCONST])
        xs = sb("xs", [128, NP, C])
        wq = sb("wq", [KC, NK, C])
        wk = sb("wk", [KC, NK, C])
        wv = sb("wv", [KC, NK, C])
        wp = sb("wp", [KC, NK, C])
        wf1 = sb("wf1", [KC, NK, FF])
        wf2 = sb("wf2", [128, NF, C])
        bqs, bks = sb("bqs", [HP, 3]), sb("bks", [HP, 3])
        bvs = sb("bvs", [128, C // 2])
        bps, bf2s = sb("bps", [128, C]), sb("bf2s", [128, C])
        bf1s = sb("bf1s", [128, NF])
        gate_a = sb("gate_a", [128, NP, C])
        adaT = sb("adaT", [KC, 4, NK, B])
        bac = sb("bac", [KC, 4, NK])
        bag = sb("bag", [1, 2, C])
        gates = sb("gates", [2 * B, C])
        cT = sb("cT", [KC, NK, B])
        sT = sb("sT", [KC, NK, B])
        eT = sb("eT", [KC, NK, B])

        areaA = sb("areaA", [128, NK * NP * 128 + 768])
        xTs = areaA[0:KC, 0:NK * 2048].rearrange("p (k t) -> p k t", k=NK)
        hx = areaA[:, 0:NF * GT].rearrange("p (n t) -> p n t", n=NF)
        hg = areaA[:, NF * GT:2 * NF * GT].rearrange("p (n t) -> p n t", n=NF)
        hs = areaA[:, 2 * NF * GT:3 * NF * GT].rearrange("p (n t) -> p n t", n=NF)
        areaB = sb("areaB", [128, NK * 6 * C])
        wada = areaB[0:KC, :].rearrange("p (k n) -> p k n", k=NK)
        Pm = areaB[:, 0:2048].rearrange("p (t n) -> p t n", t=G)
        Pt = areaB[:, 2048:4096].rearrange("p (t q r m) -> p t q r m", t=G, q=2, r=4)
        oT = areaB[0:KC, 4096:4096 + G * NK * 128].rearrange("p (g k t) -> p g k t", g=G, k=NK)
        areaC = sb("areaC", [128, NK * 2048 + 2048])
        wfold = areaC[0:KC, 0:NK * 2048].rearrange("p (k n) -> p k n", k=NK)
        bfs = areaC[0:1, NK * 2048:NK * 2048 + 2048]
        gate_m = areaC[:, 0:NP * C].rearrange("p (n c) -> p n c", n=NP)
        XY = areaC[:, NP * C:NP * C + 2048].rearrange("p (n s j) -> p n s j", n=NP, s=2)
        XD = areaB[:, 0:2048].rearrange("p (n b j) -> p n b j", n=NP, b=2)
        BD = areaB[:, 2048:4096].rearrange("p (n b j) -> p n b j", n=NP, b=2)
        areaD = sb("areaD", [128, 2048])
        Fm = areaD[:, 0:1024].rearrange("p (n j) -> p n j", n=NP)
        Am = areaD[:, 1024:2048].rearrange("p (n j) -> p n j", n=NP)
        Vb = areaD[:, 0:G * 8 * 4 * VW].rearrange("p (g n b v) -> p g n b v", g=G, n=8, b=2)
        oN = areaD[:, 1216:1216 + G * C].rearrange("p (g c) -> p g c", g=G)
        areaE = sb("areaE", [128, 2048])
        zT = areaE[:, 0:1024].rearrange("p (n t) -> p n t", n=NP)
        qT = areaE[0:HP, 0:3 * GT].rearrange("p (c t) -> p c t", c=3)
        kD = [a[0:HP].rearrange("p (r t) -> p r t", t=GT)
              for a in (areaC[:, NP * C:NP * C + 1536], areaC[:, NP * C + 1536:NP * C + 2816], areaE[:, 768:2048])]
        vB = areaD[:, 0:512]
        Ft = areaE[:, 0:1024].rearrange("p (n j) -> p n j", n=NP)
        cI = areaE[:, 1024:1664].rearrange("p (k s j) -> p k s j", k=TERMS, s=2)
        Zl = areaE[0:D, 1664:2048].rearrange("p (l j) -> p l j", l=6)
        AT = sb("AT", [D, C + 1])
        tp = sb("tp", [128, G, C])
        bc = tp[0:D, 0]
        scr = tp[0:D, 1]
        TAU = sb("TAU", [D, D])
        q_G, q_m, q_aa, q_am = (sb(n, [D, 1]) for n in ("q_G", "q_m", "q_aa", "q_am"))
        q_w, q_cf = sb("q_w", [D, 1]), sb("q_cf", [D, 1])
        q_nq, q_nqb = (sb(n, [D, 2]) for n in ("q_nq", "q_nqb"))
        NB = sb("NB", [D, D])
        tauc = sb("tauc", [D, 1])
        Vn = sb("Vn", [KC, NK, D])
        Z = sb("Z", [D, 2, D])
        Ztl = sb("Ztl", [D, 6, D])
        X = sb("X", [D, 2, D])
        P = sb("P", [D, 2, D])
        tV = sb("tV", [D, D])
        Fq = sb("Fq", [D, 2, D])
        Us = sb("Us", [KC, NK, D])
        Ut = sb("Ut", [128, C])
        hT = sb("hT", [KC, NK, GT])
        xn = sb("xn", [128, G, C])
        st = sb("st", [128, G, 6])
        mv = sb("mv", [128, G, 2])
        ve = sb("ve", [128, G])
        held = sb("held", [1, 1])
        rs = sb("rs", [128, G])
        mx = sb("mx", [128, 32])
        rden = sb("rden", [128, 4, 4, 2])

        ident = cst[:, C_ID:C_ID + 128]
        i64 = cst[0:D, C_ID:C_ID + D]

        ld_c, ld_v, ld_ada, ld_q, ld_x, ld_xt = (sem(n) for n in ("ld_c", "ld_v", "ld_ada", "ld_q", "ld_x", "ld_xt"))
        ld_w, ld_m, ld_f, ld_k = sem("ld_w"), sem("ld_m"), sem("ld_f"), sem("ld_k")
        s_silu, s_exp = sem("s_silu"), sem("s_exp")
        s_vps, s_vsb, s_bounce = sem("s_vps"), sem("s_vsb"), sem("s_bounce")
        s_ada, s_adas, s_gps, s_gsb = sem("s_ada"), sem("s_adas"), sem("s_gps"), sem("s_gsb")
        s_gbounce, ld_g, s_zero, s_ab = (sem(n) for n in ("s_gbounce", "ld_g", "s_zero", "s_ab"))
        q_ch, q_up, q_sqd, q_act, q_fin = (sem(n) for n in ("q_ch", "q_up", "q_sqd", "q_act", "q_fin"))
        s_b1, s_ft, s_mk, s_ci, e_h, e_sum = (sem(n) for n in ("s_b1", "s_ft", "s_mk", "s_ci", "e_h", "e_sum"))
        s_pe, s_dv = sem("s_pe"), sem("s_dv")
        s_am, e_pe, e_act = sem("s_am"), sem("e_pe"), sem("e_act")
        s_z, s_zs, s_w, s_ws, s_xr, s_xrs = (sem(n) for n in ("s_z", "s_zs", "s_w", "s_ws", "s_xr", "s_xrs"))
        dch = sem("dch")
        a_st, a_rs, a_xn, a_T, a_mod, a_hT = (sem(n) for n in ("a_st", "a_rs", "a_xn", "a_T", "a_mod", "a_hT"))
        a_Q, a_q, a_K, a_k, a_V, a_v = (sem(n) for n in ("a_Q", "a_q", "a_K", "a_k", "a_V", "a_v"))
        a_S, a_mx, a_sub, a_exp, a_PT, a_pt = (sem(n) for n in ("a_S", "a_mx", "a_sub", "a_exp", "a_PT", "a_pt"))
        a_PV, a_rd, a_o, a_OT, a_ot, a_Y, a_y, a_res = (sem(n) for n in (
            "a_PV", "a_rd", "a_o", "a_OT", "a_ot", "a_Y", "a_y", "a_res"))
        s_vz, s_bq = sem("s_vz"), sem("s_bq")
        m_st, m_rs, m_xn, m_T, m_mod, m_hT = (sem(n) for n in ("m_st", "m_rs", "m_xn", "m_T", "m_mod", "m_hT"))
        m_F, m_sq, m_hx, m_in, m_th, m_g = (sem(n) for n in ("m_F", "m_sq", "m_hx", "m_in", "m_th", "m_g"))
        m_Y, m_y, m_res, m_out = (sem(n) for n in ("m_Y", "m_y", "m_res", "m_out"))

        out_t = out.rearrange("(n t) c -> t n c", t=128)
        block = ctx.enter_context(nc.Block())

        @block.sync
        def _(sp):
            sp.dma_start(cT[:], condT).then_inc(ld_c, 16)
            sp.dma_start(AT[:, 0:C], PT_).then_inc(ld_q, 16)
            sp.dma_start(cst[0:D, C_NGT:C_NGT + D], consts[0:D, C_NGT:C_NGT + D]).then_inc(ld_q, 16)
            for h in range(2):
                sp.dma_start(wfold[:, :, 1024 * h:1024 * h + 1024], Wfold[:, :, 1024 * h:1024 * h + 1024]).then_inc(ld_v, 16)
            sp.dma_start(bfs, bfold).then_inc(ld_v, 16)
            sp.dma_start(cst[:, 0:C_NGT], consts[:, 0:C_NGT]).then_inc(ld_k, 16)
            sp.dma_start(cst[D:128, C_NGT:C_NGT + D], consts[D:128, C_NGT:C_NGT + D]).then_inc(ld_k, 16)
            sp.dma_start(cst[:, C_NGT + D:NCONST], consts[:, C_NGT + D:NCONST]).then_inc(ld_k, 16)
            sp.dma_start(wada, Wada).then_inc(ld_ada, 16)
            sp.dma_start(bac[:], bada_col).then_inc(ld_ada, 16)
            sp.dma_start(bag[:], bada_gate).then_inc(ld_ada, 16)
            sp.wait_ge(s_vsb, 1)
            for n in range(4):
                sp.dma_start(scratch[:, 512 * n:512 * n + 512], vB[B * n:B * n + B]).then_inc(s_bounce, 16)
            sp.wait_ge(s_bounce, 64)
            rows = scratch.rearrange("(n b) (r j) -> b r n j", b=2, j=D)
            for b in range(2):
                for half in range(2):
                    at = 64 * b + 32 * half
                    sp.dma_start(Fm[at:at + 32], rows[b]).then_inc(ld_f, 16)
            sp.dma_start(xTs, xT).then_inc(ld_xt, 16)
            sp.dma_start(xs[:], x.rearrange("(n t) c -> t n c", t=128)).then_inc(ld_x, 16)
            for t, src in ((wq, Wq), (wk, Wk), (wv, Wv), (wp, Wp), (bqs, bq), (bks, bk), (bvs, bv), (bps, bp)):
                sp.dma_start(t[:], src).then_inc(ld_w, 16)
            for t, src in ((wf1, Wf1), (wf2, Wf2), (bf1s, bf1), (bf2s, bf2)):
                sp.dma_start(t[:], src).then_inc(ld_m, 16)
            sp.wait_ge(s_gsb, 1)
            for g in range(2):
                sp.dma_start(gate_scratch[:, g], gates[B * g:B * g + B]).then_inc(s_gbounce, 16)
            sp.wait_ge(s_gbounce, 32)
            for g, tile in enumerate((gate_a, gate_m)):
                rows = gate_scratch.rearrange("(n b) g c -> g b n c", b=2)[g]
                for b in range(2):
                    sp.dma_start(tile[64 * b:64 * b + 64], rows[b].unsqueeze(0).broadcast_to([L, NP, C])
                                 ).then_inc(ld_g, 16)
            with sp.Fori(0, NG - 1) as u:
                sp.wait_ge(m_res, 2 * u + 3)
                sp.dma_start(out_t[:, bass.ds(G * u, G)], xs[:, bass.ds(G * u, G)]).then_inc(m_out, 16)
            for t in range(G):
                sp.wait_ge(m_res, 2 * NG + 1 + 2 * t)
                sp.dma_start(out_t[:, G * (NG - 1) + t], xs[:, G * (NG - 1) + t]).then_inc(m_out, 16)
            sp.wait_ge(m_out, 16 * (NG - 1 + G))

        @block.gpsimd
        def _(pool):
            pool.wait_ge(ld_ada, 48)
            for a in (1, 3):
                pool.tensor_scalar(bac[:, a], bac[:, a], 1.0, None, ALU.add).then_inc(s_b1, 1)
            pool.wait_ge(ld_k, 48)
            for k in range(TERMS):
                for s in range(2):
                    coef = float((-1) ** k / factorial(2 * k + s))
                    pool.tensor_scalar(cI[:, k, s], cst[:, C_ID2:C_ID2 + D], coef, None, ALU.mult).then_inc(s_ci, 1)
            pool.wait_ge(ld_f, 64)
            m1 = cst[:, C_M1:C_M1 + 32].unsqueeze(1).broadcast_to([128, NP, 32])
            m2 = cst[:, C_M2:C_M2 + 32].unsqueeze(1).broadcast_to([128, NP, 32])
            t1, t2 = XY[:, :, 0, 0:32], XY[:, :, 1, 0:32]
            pool.tensor_tensor(t1, Fm[:, :, 0:32], m1, ALU.mult).then_inc(s_mk, 1)
            pool.wait_ge(s_ft, 1)
            pool.tensor_tensor(t2, Ft[:, :, 0:32], m2, ALU.mult).then_inc(s_mk, 1)
            pool.wait_ge(s_mk, 2)
            for b in range(2):
                top, low = slice(64 * b, 64 * b + 32), slice(64 * b + 32, 64 * b + 64)
                pool.tensor_tensor(Am[top, :, 0:32], t1[top], t2[top], ALU.add).then_inc(s_am, 1)
                pool.wait_ge(s_am, 2 * b + 1)
                pool.tensor_tensor(Am[low, :, 32:64], t1[low], t2[low], ALU.add).then_inc(s_am, 1)
                pool.wait_ge(s_am, 2 * b + 2)
            pool.wait_ge(s_gps, 1)
            pool.memset(areaB[:, 0:4096], 0.0).then_inc(s_zero, 1)
            pool.wait_ge(s_ci, 2 * TERMS)
            for q in range(4):
                pool.wait_ge(e_act, E_ACT(0, q))
                pool.tensor_tensor(XY[:, 4 * q:4 * q + 4], XY[:, 4 * q:4 * q + 4],
                                   cI[:, TERMS - 1].unsqueeze(1).broadcast_to([128, 4, 2, D]), ALU.add).then_inc(e_h, 1)
            for q in range(4):
                pool.wait_ge(e_act, E_ACT(E_STAGES - 1, q))
                for b in range(2):
                    at = slice(64 * b, 64 * b + 64)
                    pool.tensor_tensor(BD[at, 4 * q:4 * q + 4, b], XY[at, 4 * q:4 * q + 4, 0],
                                       XY[at, 4 * q:4 * q + 4, 1], ALU.add).then_inc(e_sum, 1)
                    pool.wait_ge(e_sum, 2 * q + b + 1)

            pool.wait_ge(e_sum, 8)
            pool.wait_ge(e_act, E_ACT(E_STAGES - 1, 3))
            pool.memset(areaD[:, 0:G * 8 * 4 * VW], 0.0).then_inc(s_vz, 1)
            pool.wait_ge(s_vz, 1)
            for b in range(2):
                pool.memset(Vb[64 * b:64 * b + 64].rearrange("p g n b (h v) -> p (g n b) h v", v=VW)[:, :, b, DH], 1.0
                            ).then_inc(s_vz, 1)
                pool.wait_ge(s_vz, 2 + b)

            def rstd(stat, done, n):
                pool.wait_ge(stat, n)
                pool.tensor_tensor(rs[:], ve[:], cst[:, C_HALF:C_HALF + G], ALU.pow).then_inc(done, 1)

            def shift(mod, done, n, which, g):
                pool.wait_ge(mod, n)
                pool.tensor_tensor(hT[:].rearrange("p k (b t) -> p k b t", b=4),
                                   hT[:].rearrange("p k (b t) -> p k b t", b=4),
                                   adaT[:, which, :, bass.ds(4 * g, 4)].unsqueeze(3).broadcast_to([KC, NK, 4, L]),
                                   ALU.add).then_inc(done, 1)

            def residual(yready, done, n, g, gate):
                pool.wait_ge(yready, n)
                pool.tensor_tensor(tp[:], tp[:], gate[:, bass.ds(G * g, G)], ALU.mult).then_inc(done, 1)
                pool.wait_ge(done, 2 * n)
                pool.tensor_tensor(xs[:, bass.ds(G * g, G)], xs[:, bass.ds(G * g, G)], tp[:], ALU.add).then_inc(done, 1)

            pool.wait_ge(ld_g, 64)
            rstd(a_st, a_rs, 1)
            shift(a_mod, a_hT, 1, 0, 0)
            rstd(a_st, a_rs, 2)

            def step(g, prev, nxt, nxt2):
                if nxt:
                    shift(a_mod, a_hT, g + 2, 0, g + 1)
                if nxt2:
                    rstd(a_st, a_rs, g + 3)
                if prev:
                    residual(a_y, a_res, g, g - 1, gate_a)

            step(0, False, True, True)
            with pool.Fori(1, NG - 2) as g:
                step(g, True, True, True)
            step(NG - 2, True, True, False)
            rstd(m_st, m_rs, 1)
            step(NG - 1, True, False, False)
            shift(m_mod, m_hT, 1, 2, 0)
            rstd(m_st, m_rs, 2)

            def mstep(u, prev, nxt, nxt2):
                if nxt:
                    shift(m_mod, m_hT, u + 2, 2, u + 1)
                if nxt2:
                    rstd(m_st, m_rs, u + 3)
                if prev:
                    residual(m_y, m_res, u, u - 1, gate_m)
                else:
                    residual(a_y, a_res, NG, NG - 1, gate_a)

            mstep(0, False, True, True)
            with pool.Fori(1, NG - 2) as u:
                mstep(u, True, True, True)
            mstep(NG - 2, True, True, False)
            mstep(NG - 1, True, False, False)
            for t in range(G):
                n = G * (NG - 1) + t
                pool.wait_ge(m_y, NG + t)
                pool.tensor_tensor(tp[:, t], tp[:, t], gate_m[:, n], ALU.mult).then_inc(m_res, 1)
                pool.wait_ge(m_res, 2 * NG + 2 * t)
                pool.tensor_tensor(xs[:, n], xs[:, n], tp[:, t], ALU.add).then_inc(m_res, 1)

        @block.scalar
        def _(act):
            act.wait_ge(ld_c, 16)
            nc.scalar.activation(eT[:], cT[:], ACT.Exp, scale=-1.0).then_inc(s_exp, 1)

            def skew_out():
                act.wait_ge(s_vps, 1)
                nc.scalar.activation(vB, ps[:, 0, :], ACT.Copy, scale=1.0 / (1 << SQUARINGS)).then_inc(s_vsb, 1)

            def ada_out(a):
                if a == 0:
                    act.wait_ge(s_ada, 1)
                    act.wait_ge(s_b1, 2)
                for k in range(NK):
                    at = 32 * (NK * a + k)
                    nc.scalar.activation(adaT[:, a, k], ps[0:KC, 4, at:at + 32], ACT.Identity,
                                         bias=bac[:, a, k:k + 1]).then_inc(s_adas, 1)

            def gates_out():
                act.wait_ge(s_gps, 1)
                nc.scalar.activation(gates[:], ps[0:2 * B, 5, 0:C], ACT.Copy).then_inc(s_gsb, 1)

            def exp_out(stage, q):
                act.wait_ge(e_pe, 4 * stage + q + 1)
                src = ps[:, q, :].rearrange("p (n s j) -> p n s j", n=4, s=2)
                quarter = slice(4 * q, 4 * q + 4)
                def diagonal(tile, half):
                    for b in range(2):
                        at = slice(64 * b, 64 * b + 64)
                        nc.scalar.activation(tile[at, quarter, b], half[at], ACT.Copy,
                                             scale=2.0 if stage == TERMS - 1 else 1.0).then_inc(e_act, 1)

                if stage == 0:
                    src = ps[:, q, 0:4 * D].rearrange("p (n j) -> p n j", n=4)
                    for s in range(2):
                        coef = float((-1) ** TERMS / factorial(2 * TERMS + s))
                        nc.scalar.activation(XY[:, quarter, s], src, ACT.Copy, scale=coef).then_inc(e_act, 1)
                    diagonal(BD, src)
                elif stage == TERMS - 1:
                    nc.scalar.activation(XY[:, quarter], src, ACT.Copy, scale=2.0).then_inc(e_act, 1)
                    diagonal(XD, src[:, :, 0])
                elif stage == TERMS:
                    src = ps[:, q, 0:4 * D].rearrange("p (n j) -> p n j", n=4)
                    nc.scalar.activation(XY[:, quarter, 1], src, ACT.Copy, scale=-1.0).then_inc(e_act, 1)
                else:
                    nc.scalar.activation(XY[:, quarter], src, ACT.Copy).then_inc(e_act, 1)
                    if TERMS < stage < E_STAGES - 1:
                        diagonal(XD, src[:, :, 0])

            def skew_blocks(b):
                top, low = slice(64 * b, 64 * b + 32), slice(64 * b + 32, 64 * b + 64)
                nc.scalar.activation(Am[top, :, 32:64], Fm[top, :, 32:64], ACT.Copy).then_inc(s_ab, 1)
                nc.scalar.activation(Am[low, :, 0:32], Ft[low, :, 32:64], ACT.Copy, scale=-1.0).then_inc(s_ab, 1)

            act.wait_ge(ld_q, 32)
            for j in range(D):
                act.wait_ge(q_up, j + 1)
                rows = slice(32 * (j // 32), 32 * (j // 32) + 32)
                nc.scalar.activation(hT[rows, 0:2].rearrange("p k t -> p (k t)")[:, j:C + 1], AT[rows, j:C + 1], ACT.Square,
                                     accum_out=q_nq[rows, 0:1]).then_inc(q_sqd, 1)
                act.wait_ge(q_sqd, j + 1)
                nc.scalar.activation(q_nq[rows, 1:2], q_nq[rows, 0:1], ACT.Sqrt, scale=4.0).then_inc(q_act, 1)
                if j == SKEW_AT:
                    skew_out()
                if ADA_AT <= j < ADA_AT + 4:
                    ada_out(j - ADA_AT)
                if j == ADA_AT + 4:
                    gates_out()
                if j == FOLD_AT + 1:
                    act.wait_ge(ld_f, 64)
                    act.wait_ge(s_ft, 1)
                    skew_blocks(0)
                if j == FOLD_AT + 2:
                    skew_blocks(1)
                if j == E_FIRST:
                    act.wait_ge(s_zero, 1)
                for piece in range(E_BEFORE(j), E_BEFORE(j + 1)):
                    exp_out(piece // 4, piece % 4)

            def q_out(n):
                act.wait_ge(a_Q, n)
                for c, (h0, h1) in enumerate(HEADS):
                    at = slice(0, DH * (h1 - h0))
                    nc.scalar.activation(qT[at, c], ps[at, 6 + c // 2, 256 * (c % 2):256 * (c % 2) + 256],
                                         ACT.Identity, bias=bqs[at, c:c + 1], scale=float(DH) ** -0.5).then_inc(a_q, 1)

            def ot_out(n):
                act.wait_ge(a_OT, n)
                for g in range(G):
                    nc.scalar.activation(oT[:, g].rearrange("p k t -> p (k t)"), ps[0:KC, 6 + g, 0:NK * 128],
                                         ACT.Copy).then_inc(a_ot, 1)

            def exps(n):
                for t in range(G):
                    act.wait_ge(a_sub, 4 * n - 2 + 2 * t)
                    nc.scalar.activation(Pm[:, t], Pm[:, t], ACT.Exp).then_inc(a_exp, 1)

            def pt_out(n):
                for i in range(4):
                    act.wait_ge(a_PT, 4 * n - 3 + i)
                    nc.scalar.activation(Pt[:, i // 2, i % 2].rearrange("p r m -> p (r m)"), ps[:, i, :],
                                         ACT.Copy).then_inc(a_pt, 1)

            act.wait_ge(ld_w, 16 * 8)
            act.wait_ge(s_bq, 1)
            q_out(1)

            def step(g, prev, nxt):
                if prev:
                    ot_out(g)
                exps(g + 1)
                pt_out(g + 1)
                if nxt:
                    q_out(g + 2)

            step(0, False, True)
            with act.Fori(1, NG - 1) as g:
                step(g, True, True)
            step(NG - 1, True, False)
            ot_out(NG)

            act.wait_ge(ld_m, 16 * 4)

            def mstep(u, prev, parts=WHOLE):
                if prev:
                    act.wait_ge(m_g, u)
                for j in range(5):
                    act.wait_ge(m_F, 5 * u + j + 1)
                    for c in range(2 * j, min(2 * j + 2, NF)):
                        ins = nc.scalar.activation(hs[:, c], ps[:, j % 4, 256 * (c % 2):256 * (c % 2) + 256],
                                                   ACT.Square, bias=bf1s[:, c:c + 1])
                    ins.then_inc(m_sq, 1)
                for part, tok in enumerate(parts):
                    act.wait_ge(m_in, 2 * u + 2 + 2 * part)
                    nc.scalar.activation(hs[:, :, tok], hs[:, :, tok], ACT.Tanh, scale=GELU_C).then_inc(m_th, 1)

            mstep(0, False)
            with act.Fori(1, NG - 1) as u:
                mstep(u, True)
            mstep(NG - 1, True, PAIRS)

        @block.vector
        def _(dve):
            v = nc.vector
            count = [0]

            def link(ins):
                count[0] += 1
                ins.then_inc(dch, 1)
                dve.wait_ge(dch, count[0])

            dve.wait_ge(s_exp, 1)
            link(v.tensor_scalar(eT[:], eT[:], 1.0, None, ALU.add))
            link(v.reciprocal(eT[:], eT[:]))
            v.tensor_tensor(sT[:], eT[:], cT[:], ALU.mult).then_inc(s_silu, 1)
            steps = [0]

            def qr(ins):
                steps[0] += 1
                ins.then_inc(q_ch, 1)
                return steps[0]

            v.memset(TAU[:], 1.0).then_inc(q_ch, 1)
            v.memset(NB[:], 0.0).then_inc(q_ch, 1)
            v.memset(AT[:, C:C + 1], 1e-15).then_inc(q_up, 1)
            steps[0] = 2
            dve.wait_ge(ld_q, 32)
            dve.wait_ge(q_ch, 2)
            for j in range(D):
                rows = slice(0, D) if j < 32 else slice(32, D)
                src = slice(32 * (j // 32), 32 * (j // 32) + 32)
                spread = (0, 32) if j < 32 else (32,)
                a, tail = AT[rows], bc[rows]
                below = cst[rows, C_NGT + j:C_NGT + j + 1]
                tau = TAU[rows, j:j + 1]
                dve.wait_ge(q_up, j + 1)
                for at in spread:
                    n = qr(v.stream_shuffle(bc[at:at + 32, j:C], AT[src, j:C], [j % 32] * 32))
                dve.wait_ge(q_ch, n)
                qr(v.tensor_scalar(q_m[rows], tail[:, j:j + 1], 0.0, -0.5, ALU.is_ge, ALU.add))
                dots = qr(v.tensor_tensor_reduce(out=scr[rows, j:C], in0=a[:, j:C], in1=tail[:, j:C], scale=1.0, scalar=0.0,
                                                 op0=ALU.mult, op1=ALU.add, accum_out=q_G[rows]))
                dve.wait_ge(q_act, j + 1)
                for at in spread:
                    n = qr(v.stream_shuffle(q_nqb[at:at + 32], q_nq[src], [j % 32] * 32))
                dve.wait_ge(q_ch, dots)
                qr(v.tensor_tensor(q_aa[rows], tail[:, j:j + 1], q_m[rows], ALU.mult))
                n = qr(v.tensor_tensor(q_am[rows], a[:, j:j + 1], q_m[rows], ALU.mult))
                dve.wait_ge(q_ch, n)
                n = qr(v.scalar_tensor_tensor(out=tau, in0=q_aa[rows], scalar=q_nqb[rows, 1:2], in1=q_nqb[rows, 0:1],
                                              op0=ALU.mult, op1=ALU.add))
                qr(v.scalar_tensor_tensor(out=q_w[rows], in0=q_am[rows], scalar=q_nqb[rows, 1:2], in1=q_G[rows],
                                              op0=ALU.mult, op1=ALU.add))
                dve.wait_ge(q_ch, n)
                n = qr(v.reciprocal(tau, tau))
                qr(v.tensor_tensor(NB[rows, j:j + 1], q_m[rows], q_nqb[rows, 1:2], ALU.mult))
                if j < D - 1:
                    dve.wait_ge(q_ch, n)
                    n = qr(v.scalar_tensor_tensor(out=q_cf[rows], in0=q_w[rows], scalar=tau, in1=below,
                                                  op0=ALU.mult, op1=ALU.mult))
                    dve.wait_ge(q_ch, n)
                    v.scalar_tensor_tensor(out=a[:, j + 1:C], in0=tail[:, j + 1:C], scalar=q_cf[rows, 0:1],
                                           in1=a[:, j + 1:C], op0=ALU.mult, op1=ALU.add).then_inc(q_up, 1)
                if j == FOLD_AT:
                    dve.wait_ge(ld_f, 64)
                    v.transpose(Ft.rearrange("p n j -> p (n j)"), Fm.rearrange("p n j -> p (n j)")).then_inc(s_ft, 1)
            dve.wait_ge(ld_k, 48)
            dve.wait_ge(q_ch, steps[0])
            v.tensor_tensor(NB[:], NB[:], i64, ALU.mult).then_inc(q_fin, 1)
            v.tensor_tensor(AT[:, 0:D], AT[:, 0:D], cst[0:D, C_LE:C_LE + D], ALU.mult).then_inc(q_fin, 1)
            dve.wait_ge(q_fin, 2)
            v.tensor_tensor(AT[:, 0:D], AT[:, 0:D], NB[:], ALU.add).then_inc(q_fin, 1)
            dve.wait_ge(q_fin, 3)

            link(v.tensor_tensor_reduce(out=scr[:, 0:D], in0=TAU[:], in1=i64, scale=1.0, scalar=0.0, op0=ALU.mult,
                                        op1=ALU.add, accum_out=tauc[:]))
            dve.wait_ge(s_pe, 1)
            v.tensor_copy(Vn[:], ps[0:KC, 0, 0:NK * D].rearrange("p (k d) -> p k d", k=NK)).then_inc(s_dv, 1)
            link(v.tensor_scalar(tV[:], AT[:, 0:D], tauc[:, 0:1], None, ALU.mult))
            dve.wait_ge(s_pe, 2)
            link(v.tensor_scalar(Z[:, 0], ps[0:D, 1, 0:D], tauc[:, 0:1], None, ALU.mult))
            link(v.tensor_tensor(Z[:, 1], ps[0:D, 1, 0:D], TAU[:], ALU.mult))
            for s, masks in enumerate((C_LV, C_LVT)):
                v.tensor_tensor((Zl, Ztl)[s][:], Z[:, s].unsqueeze(1).broadcast_to([D, 6, D]),
                                cst[0:D, masks:masks + 384].rearrange("p (l j) -> p l j", l=6), ALU.mult).then_inc(s_dv, 1)
            dve.wait_ge(s_dv, 3)
            v.tensor_tensor(X[:, 0], i64, Zl[:, 0], ALU.subtract).then_inc(s_dv, 1)
            v.tensor_tensor(X[:, 1], i64, Ztl[:, 0], ALU.subtract).then_inc(s_dv, 1)
            for level in range(1, 6):
                dve.wait_ge(s_pe, 2 * level + 1)
                v.tensor_copy(P[:], ps[0:D, 0, 0:2 * D].rearrange("p (s d) -> p s d", s=2)).then_inc(s_dv, 1)
                dve.wait_ge(s_pe, 2 * level + 2)
                v.tensor_tensor(X[:], X[:], ps[0:D, 1, 0:2 * D].rearrange("p (s d) -> p s d", s=2),
                                ALU.subtract).then_inc(s_dv, 1)
            dve.wait_ge(s_pe, 13)
            v.tensor_copy(Fq[:], ps[0:D, 2, 0:D].unsqueeze(1).broadcast_to([D, 2, D])).then_inc(s_dv, 1)
            dve.wait_ge(s_pe, 14)
            v.tensor_tensor(Us[:, 0], cst[0:KC, C_ID:C_ID + D], ps[0:KC, 3, 0:D], ALU.subtract).then_inc(s_dv, 1)
            v.tensor_scalar(Us[:, 1:3], ps[0:KC, 3, D:3 * D].rearrange("p (k d) -> p k d", k=2), -1.0, None,
                            ALU.mult).then_inc(s_dv, 1)
            v.tensor_scalar(Ut[:], ps[:, 4, 0:C], -1.0, None, ALU.mult).then_inc(s_dv, 1)
            dve.wait_ge(s_dv, 19)
            v.tensor_tensor(Ut[:, 0:D], Ut[:, 0:D], cst[:, C_ID2:C_ID2 + D], ALU.add).then_inc(s_dv, 1)

            for h in range(2):
                dve.wait_ge(s_z, h + 1)
                v.tensor_copy(zT[:, 8 * h:8 * h + 8], ps[:, 4 + h, :].rearrange("p (n t) -> p n t", n=8)).then_inc(s_zs, 1)

            def w_out(h):
                dve.wait_ge(s_w, h + 1)
                for b in range(2):
                    at = slice(64 * b, 64 * b + 64)
                    v.tensor_scalar(XD[at, 8 * h:8 * h + 8, b],
                                    ps[at, (6, 4)[h], :].rearrange("p (n t) -> p n t", n=8),
                                    0.5, None, ALU.mult).then_inc(s_ws, 1)

            w_out(0)
            dve.wait_ge(ld_x, 16)

            def rotated(n):
                dve.wait_ge(s_xr, n + 1)
                v.tensor_tensor(xs[:, n], xs[:, n], ps[:, n % 4, 0:C], ALU.add).then_inc(s_xrs, 1)

            dve.wait_ge(ld_w, 16 * 8)
            v.tensor_scalar(bqs[:], bqs[:], float(DH) ** -0.5, None, ALU.mult).then_inc(s_bq, 1)

            def stats(stat, rstd, xnd, n, g):
                for t in range(G):
                    v.bn_stats(st[:, t], xs[:, bass.ds(G * g + t, 1)].rearrange("p a c -> p (a c)")).then_inc(stat[1], 1)
                dve.wait_ge(stat[1], 5 * n - 3)
                v.memset(held[:], 0.0).then_inc(stat[1], 1)
                for t in range(G):
                    v.bn_aggr(mv[:, t], st[:, t]).then_inc(stat[1], 1)
                dve.wait_ge(stat[1], 5 * n)
                v.tensor_scalar(ve[:], mv[:, :, 1], LN_EPS, None, ALU.add).then_inc(stat[0], 1)
                dve.wait_ge(rstd, n)
                for t in range(G):
                    v.tensor_scalar(xn[:, t], xs[:, bass.ds(G * g + t, 1)].rearrange("p a c -> p (a c)"),
                                    mv[:, t, 0:1], rs[:, t:t + 1], ALU.subtract, ALU.mult).then_inc(xnd, 1)

            def scale(T, mod, n, which, g, bank):
                dve.wait_ge(T, n)
                src = ps[0:KC, bank:bank + 2, :].rearrange("p b n -> p (b n)")[:, 0:NK * GT].rearrange(
                    "p (k b t) -> p k b t", k=NK, b=4)
                v.tensor_tensor(hT[:].rearrange("p k (b t) -> p k b t", b=4), src,
                                adaT[:, which, :, bass.ds(4 * g, 4)].unsqueeze(3).broadcast_to([KC, NK, 4, L]),
                                ALU.mult).then_inc(mod, 1)

            def k_out(n, chunks):
                for c in chunks:
                    dve.wait_ge(a_K, n)
                    heads = HEADS[c][1] - HEADS[c][0]
                    at = slice(0, DH * heads)
                    shape = [DH * heads, heads, GT]
                    src = ps[at, 4 + c // 2, 256 * (c % 2):256 * (c % 2) + 256]
                    v.scalar_tensor_tensor(out=kD[c][at], in0=src.unsqueeze(1).broadcast_to(shape), scalar=bks[at, c:c + 1],
                                           in1=cst[at, C_HM:C_HM + heads].unsqueeze(2).broadcast_to(shape),
                                           op0=ALU.add, op1=ALU.mult).then_inc(a_k, 1)

            def v_out(n):
                dve.wait_ge(a_V, n)
                for g in range(G):
                    for h in range(2):
                        at = slice(64 * h, 64 * h + 64)
                        v.tensor_tensor(
                            Vb[at, g].rearrange("p n b (h v) -> p n b h v", v=VW)[:, :, :, h, 0:DH],
                            ps[at, 4 + g, 0:C].rearrange("p (b n d) -> p n b d", b=2, n=8),
                            bvs[at].rearrange("p (n d) -> p n d", n=8).unsqueeze(2).broadcast_to([64, 8, 2, DH]),
                            ALU.add).then_inc(a_v, 1)

            def maxima(n):
                dve.wait_ge(a_S, n)
                v.tensor_reduce(mx[:].rearrange("p (e r) -> p e r", e=4), ps[:, 0:4, :].rearrange("p e (r m) -> p e r m", m=L),
                                AX.X, ALU.max).then_inc(a_mx, 1)
                dve.wait_ge(a_mx, n)
                for e in range(4):
                    v.tensor_tensor(Pm[:, e // 2, 512 * (e % 2):512 * (e % 2) + 512].rearrange("p (r m) -> p r m", m=L),
                                    ps[:, e, :].rearrange("p (r m) -> p r m", m=L),
                                    mx[:, 8 * e:8 * e + 8].unsqueeze(2).broadcast_to([128, 8, L]),
                                    ALU.subtract).then_inc(a_sub, 1)

            def norm(n):
                for g in range(G):
                    dve.wait_ge(a_PV, 2 * n - 1 + g)
                    for b in range(2):
                        at = slice(64 * b, 64 * b + 64)
                        src = ps[at, 4 + 2 * g:6 + 2 * g, 0:304].rearrange("p q (r b h v) -> p q r b h v", r=4, b=2, h=2)
                        for q in range(2):
                            v.reciprocal(rden[at, 2 * g + q], src[:, q, :, b, :, DH]).then_inc(a_rd, 1)
                    dve.wait_ge(a_rd, 8 * n - 4 + 4 * g)
                    for b in range(2):
                        at = slice(64 * b, 64 * b + 64)
                        for q in range(2):
                            src = ps[at, 4 + 2 * g + q, 0:304].rearrange("p (r b h v) -> p r b h v", r=4, b=2, h=2)
                            v.tensor_tensor(
                                oN[at, g, 144 * q:144 * q + 144].rearrange("p (r h d) -> p r h d", r=4, h=2),
                                src[:, :, b, :, 0:DH], rden[at, 2 * g + q].unsqueeze(3).broadcast_to([64, 4, 2, DH]),
                                ALU.mult).then_inc(a_o, 1)

            def proj_out(Y, y, res, n, bank, bias, half):
                dve.wait_ge(res, 2 * n - 1)
                dve.wait_ge(Y, G * n)
                if half is None:
                    v.tensor_tensor(tp[:], ps[:, bank:bank + 2, 0:C], bias[:].unsqueeze(1).broadcast_to([128, G, C]),
                                    ALU.add).then_inc(y, 1)
                else:
                    v.scalar_tensor_tensor(out=tp[:], in0=ps[:, bank:bank + 2, 0:C], scalar=half,
                                           in1=bias[:].unsqueeze(1).broadcast_to([128, G, C]),
                                           op0=ALU.mult, op1=ALU.add).then_inc(y, 1)

            v.memset(tp[:, 0, 0:1], 0.0).then_inc(a_res, 1)
            v.memset(tp[:, 1, 0:1], 0.0).then_inc(m_res, 1)
            A_ST = (a_st, sem("a_bn"))
            for n in range(G):
                rotated(n)
            dve.wait_ge(s_xrs, G)
            stats(A_ST, a_rs, a_xn, 1, 0)
            for n in range(G, NP // 2):
                rotated(n)
            scale(a_T, a_mod, 1, 1, 0, 6)
            w_out(1)
            dve.wait_ge(s_xrs, NP // 2)
            stats(A_ST, a_rs, a_xn, 2, 1)
            dve.wait_ge(s_vz, 3)
            k_out(1, (0, 1, 2))
            for n in range(NP // 2, NP):
                rotated(n)
            dve.wait_ge(s_xrs, NP)
            v_out(1)

            M_ST = (m_st, sem("m_bn"))

            def step(g, prev, nxt, nxt2):
                if nxt:
                    dve.wait_ge(a_V, g + 1)
                    scale(a_T, a_mod, g + 2, 1, g + 1, 6)
                else:
                    stats(M_ST, m_rs, m_xn, 1, 0)
                if nxt2:
                    stats(A_ST, a_rs, a_xn, g + 3, g + 2)
                maxima(g + 1)
                if nxt:
                    k_out(g + 2, (0,))
                if prev:
                    proj_out(a_Y, a_y, a_res, g, 6, bps, None)
                if nxt:
                    k_out(g + 2, (1, 2))
                norm(g + 1)
                if nxt:
                    v_out(g + 2)

            step(0, False, True, True)
            with dve.Fori(1, NG - 2) as g:
                step(g, True, True, True)
            step(NG - 2, True, True, False)
            step(NG - 1, True, False, False)

            dve.wait_ge(ld_m, 16 * 4)
            dve.wait_ge(a_V, NG)
            scale(m_T, m_mod, 1, 3, 0, 4)
            stats(M_ST, m_rs, m_xn, 2, 1)

            def mstep(u, prev, nxt, nxt2, parts=WHOLE):
                for j in range(5):
                    dve.wait_ge(m_sq, 5 * u + j + 1)
                    for c in range(2 * j, min(2 * j + 2, NF)):
                        ins = v.tensor_scalar(hx[:, c], ps[:, j % 4, 256 * (c % 2):256 * (c % 2) + 256],
                                              bf1s[:, c:c + 1], None, ALU.add)
                        ins.then_inc(m_hx, 1)
                if nxt:
                    scale(m_T, m_mod, u + 2, 3, u + 1, 4)
                for part, tok in enumerate(parts):
                    v.tensor_scalar(hs[:, :, tok], hs[:, :, tok], GELU_A, 1.0, ALU.mult, ALU.add).then_inc(m_in, 1)
                    dve.wait_ge(m_in, 2 * u + 1 + 2 * part)
                    if part == 0:
                        dve.wait_ge(m_hx, 9 * u + 9)
                    v.tensor_tensor(hs[:, :, tok], hs[:, :, tok], hx[:, :, tok], ALU.mult).then_inc(m_in, 1)
                if nxt2:
                    stats(M_ST, m_rs, m_xn, u + 3, u + 2)
                if prev:
                    proj_out(m_Y, m_y, m_res, u, 6, bf2s, 0.5)
                else:
                    proj_out(a_Y, a_y, a_res, NG, 6, bps, None)
                for part, tok in enumerate(parts):
                    dve.wait_ge(m_th, u + 1 + part)
                    v.scalar_tensor_tensor(out=hg[:, :, tok], in0=hs[:, :, tok], scalar=1.0, in1=hx[:, :, tok],
                                           op0=ALU.add, op1=ALU.mult).then_inc(m_g, 1)

            mstep(0, False, True, True)
            dve.wait_ge(a_res, 2 * NG + 1)
            with dve.Fori(1, NG - 2) as u:
                mstep(u, True, True, True)
            mstep(NG - 2, True, True, False)
            mstep(NG - 1, True, False, False, PAIRS)
            dve.wait_ge(m_res, 2 * NG - 1)
            for t in range(G):
                dve.wait_ge(m_Y, G * NG - 1 + t)
                v.scalar_tensor_tensor(out=tp[:, t], in0=ps[:, 6 + t, 0:C], scalar=0.5, in1=bf2s[:],
                                       op0=ALU.mult, op1=ALU.add).then_inc(m_y, 1)

        @block.tensor
        def _(pe):
            def mm(out_, lhsT, rhs, first=True, last=True):
                return nc.tensor.matmul(out_, lhsT, rhs, start=first, stop=last)

            ones = cst[0:1, C_ONES:C_ONES + B]
            pe.wait_ge(ld_k, 48)
            pe.wait_ge(ld_q, 32)
            pe.wait_ge(s_silu, 1)
            pe.wait_ge(ld_v, 48)
            for k in range(NK + 1):
                for n in range(4):
                    lhsT, rhs = (sT[:, k], wfold[:, k, 512 * n:512 * n + 512]) if k < NK else (
                        ones, bfs[:, 512 * n:512 * n + 512])
                    ins = mm(ps[B * n:B * n + B, 0, :], lhsT, rhs, k == 0, k == NK)
            ins.then_inc(s_vps, 1)
            pe.wait_ge(ld_ada, 48)
            for a, part in enumerate((0, 1, 3, 4)):
                for c in range(NK):
                    for k in range(NK):
                        col = part * C + c * KC
                        ins = mm(ps[0:KC, 4, 32 * (NK * a + c):32 * (NK * a + c) + 32], wada[:, k, col:col + KC],
                                 sT[:, k], k == 0, k == NK - 1)
            ins.then_inc(s_ada, 1)
            for k in range(NK + 1):
                for n, part in enumerate((2, 5)):
                    lhsT, rhs = (sT[:, k], wada[:, k, part * C:part * C + C]) if k < NK else (ones, bag[:, n])
                    ins = mm(ps[B * n:B * n + B, 5, 0:C], lhsT, rhs, k == 0, k == NK)
            ins.then_inc(s_gps, 1)

            def product(left, right, width, q, added):
                for lhs, rhs, out_ in added:
                    nc.tensor.matmul(out_, lhs, rhs, start=rhs is added[0][1], stop=False, skip_group_check=True)
                for n in range(4):
                    for b in range(2):
                        at = slice(64 * b, 64 * b + 64)
                        lhsT, rhs = (left[at, 4 * q + n], right[at, 4 * q + n]) if left is Am else (
                            left[:, 4 * q + n, b], right[:, 4 * q + n].rearrange("p s j -> p (s j)"))
                        ins = nc.tensor.matmul(ps[at, q, width * n:width * n + width], lhsT, rhs,
                                               start=not added and n == 0, stop=True, skip_group_check=True)
                ins.then_inc(e_pe, 1)

            pe.wait_ge(s_am, 4)
            pe.wait_ge(s_ab, 4)
            pe.wait_ge(s_vsb, 1)
            for stage in range(E_STAGES):
                for q in range(4):
                    bank = ps[:, q, :].rearrange("p (n s j) -> p n s j", n=4, s=2)
                    mine = slice(4 * q, 4 * q + 4)
                    if stage == 0:
                        product(Am, Am, D, q, [])
                        continue
                    if stage == 1:
                        pe.wait_ge(e_h, q + 1)
                        pe.wait_ge(e_act, E_ACT(0, q))
                    else:
                        pe.wait_ge(e_act, E_ACT(stage - 1, q))
                    if stage < TERMS:
                        k = TERMS - 1 - stage
                        added = [] if k == 0 else [
                            (ident, cI[:, k].unsqueeze(1).broadcast_to([128, 4, 2, D]), bank)]
                        product(BD, XY, 2 * D, q, added)
                    elif stage == TERMS:
                        product(Am, XY[:, :, 1], D, q,
                                [(cst[:, C_N2I:C_N2I + 128], Am[:, mine], ps[:, q, 0:4 * D].rearrange("p (n j) -> p n j", n=4))])
                    else:
                        product(XD, XY, 2 * D, q,
                                [(cst[:, C_4I:C_4I + 128], XY[:, mine, 0], bank[:, :, 0]),
                                 (cst[:, C_2I:C_2I + 128], XY[:, mine, 1], bank[:, :, 1])])

            pe.wait_ge(q_fin, 3)
            pe.wait_ge(s_adas, 4 * NK)
            pe.wait_ge(s_gsb, 1)
            pe.wait_ge(e_act, E_ACT(E_STAGES - 1, 3))
            for k in range(NK):
                ins = nc.tensor.transpose(ps[0:KC, 0, D * k:D * k + D], AT[:, KC * k:KC * k + KC], i64)
            ins.then_inc(s_pe, 1)
            pe.wait_ge(s_dv, 1)
            for k in range(NK):
                ins = mm(ps[0:D, 1, 0:D], Vn[:, k], Vn[:, k], k == 0, k == NK - 1)
            ins.then_inc(s_pe, 1)
            for level in range(1, 6):
                pe.wait_ge(s_dv, 5 + 2 * (level - 1))
                mm(ps[0:D, 0, 0:D], Ztl[:, level], X[:, 0])
                mm(ps[0:D, 0, D:2 * D], Zl[:, level], X[:, 1]).then_inc(s_pe, 1)
                pe.wait_ge(s_dv, 6 + 2 * (level - 1))
                mm(ps[0:D, 1, 0:D], X[:, 1], P[:, 0])
                mm(ps[0:D, 1, D:2 * D], X[:, 0], P[:, 1]).then_inc(s_pe, 1)
            pe.wait_ge(s_dv, 15)
            mm(ps[0:D, 2, 0:D], X[:, 1], tV[:]).then_inc(s_pe, 1)
            pe.wait_ge(s_dv, 16)
            for k in range(NK):
                mm(ps[0:KC, 3, D * k:D * k + D], AT[:, KC * k:KC * k + KC], Fq[:, 0])
            mm(ps[:, 4, 0:C], Fq[:].rearrange("p a b -> p (a b)"), AT[:, 0:C]).then_inc(s_pe, 1)

            pe.wait_ge(s_dv, 20)
            pe.wait_ge(ld_xt, 16)
            for h in range(2):
                for k in range(NK):
                    for b in range(2):
                        rhs = xTs[:, k].rearrange("p (n b t) -> p b n t", b=2, t=L)[:, b, 8 * h:8 * h + 8]
                        ins = mm(ps[64 * b:64 * b + 64, 4 + h, :], Us[:, k], rhs, k == 0, k == NK - 1)
                ins.then_inc(s_z, 1)
            pe.wait_ge(e_sum, 8)

            def turned(h):
                pe.wait_ge(s_zs, h + 1)
                for n in range(8 * h, 8 * h + 8):
                    for b in range(2):
                        at = slice(64 * b, 64 * b + 64)
                        ins = mm(ps[at, (6, 4)[h], L * (n % 8):L * (n % 8) + L], BD[:, n, b], zT[:, n])
                ins.then_inc(s_w, 1)

            def back(h):
                pe.wait_ge(s_ws, 2 * h + 2)
                for n in range(8 * h, 8 * h + 8):
                    if n >= 4:
                        pe.wait_ge(s_xrs, n - 3)
                    mm(ps[:, n % 4, 0:C], XD[:, n].rearrange("p b t -> p (b t)"), Ut[:]).then_inc(s_xr, 1)

            turned(0)
            back(0)

            def turn(xnd, T, n, bank):
                pe.wait_ge(xnd, G * n)
                flat = ps[0:KC, bank:bank + 2, :].rearrange("p b n -> p (b n)")
                for k in range(NK):
                    for t in range(G):
                        ins = nc.tensor.transpose(flat[:, GT * k + 128 * t:GT * k + 128 * t + 128],
                                                  xn[:, t, KC * k:KC * k + KC], ident)
                ins.then_inc(T, 1)

            def qk(w, bank, ready, n):
                for c, (h0, h1) in enumerate(HEADS):
                    for k in range(NK):
                        ins = mm(ps[0:DH * (h1 - h0), bank + c // 2, 256 * (c % 2):256 * (c % 2) + 256],
                                 w[:, k, DH * h0:DH * h1], hT[:, k], k == 0, k == NK - 1)
                ins.then_inc(ready, 1)

            def values(n):
                for t in range(G):
                    for b in range(2):
                        tok = slice(128 * t + 64 * b, 128 * t + 64 * b + 64)
                        for k in range(NK):
                            for h in range(2):
                                ins = mm(ps[64 * h:64 * h + 64, 4 + t, 144 * b:144 * b + 144], hT[:, k, tok],
                                         wv[:, k, 144 * h:144 * h + 144], k == 0, k == NK - 1)
                ins.then_inc(a_V, 1)

            def scores(n):
                pe.wait_ge(a_q, 3 * n)
                pe.wait_ge(a_k, 3 * n)
                for t in range(G):
                    for c, h0, h1 in PIECES:
                        first, rows = HEADS[c][0], slice(0, DH * (HEADS[c][1] - HEADS[c][0]))
                        for b in range(2):
                            tok = slice(128 * t + 64 * b, 128 * t + 64 * b + 64)
                            ins = mm(ps[64 * b:64 * b + 64, 2 * t + h0 // 8, L * (h0 % 8):L * (h0 % 8) + L * (h1 - h0)],
                                     qT[rows, c, tok],
                                     kD[c][rows, h0 - first:h1 - first, tok])
                ins.then_inc(a_S, 1)

            def turn_out(n):
                pe.wait_ge(a_o, 8 * n)
                for g in range(G):
                    for k in range(NK):
                        ins = nc.tensor.transpose(ps[0:KC, 6 + g, 128 * k:128 * k + 128],
                                                  oN[:, g, KC * k:KC * k + KC], ident)
                ins.then_inc(a_OT, 1)

            def project(n):
                pe.wait_ge(a_ot, 2 * n)
                for t in range(G):
                    for k in range(NK):
                        ins = mm(ps[:, 6 + t, 0:C], oT[:, t, k], wp[:, k], k == 0, k == NK - 1)
                    ins.then_inc(a_Y, 1)

            def turn_p(n):
                for t in range(G):
                    pe.wait_ge(a_exp, 2 * n - 1 + t)
                    for q in range(2):
                        for r in range(4):
                            ins = nc.tensor.transpose(ps[:, 2 * t + q, 128 * r:128 * r + 128],
                                                      Pm[:, t, 512 * q + 128 * r:512 * q + 128 * r + 128], ident)
                        ins.then_inc(a_PT, 1)

            def pv(n, g):
                pe.wait_ge(a_pt, 4 * n - 2 + 2 * g)
                if g == 0:
                    pe.wait_ge(a_v, 4 * n)
                for q in range(2):
                    for r in range(4):
                        ins = mm(ps[:, 4 + 2 * g + q, 4 * VW * r:4 * VW * r + 4 * VW], Pt[:, g, q, r],
                                 Vb[:, g, 4 * q + r].rearrange("p b v -> p (b v)"))
                ins.then_inc(a_PV, 1)

            pe.wait_ge(s_vz, 3)
            pe.wait_ge(ld_w, 16 * 8)
            turn(a_xn, a_T, 1, 6)
            turned(1)
            pe.wait_ge(s_ws, 4)
            pe.wait_ge(a_hT, 1)
            qk(wk, 4, a_K, 1)
            qk(wq, 6, a_Q, 1)
            back(1)
            pe.wait_ge(a_k, 3)
            values(1)
            pe.wait_ge(a_q, 3)
            turn(a_xn, a_T, 2, 6)
            pe.wait_ge(s_xrs, NP)

            def step(g, prev, nxt, nxt2):
                scores(g + 1)
                if prev:
                    if nxt:
                        pe.wait_ge(a_mod, g + 2)
                    turn_out(g)
                if nxt:
                    pe.wait_ge(a_v, 4 * (g + 1))
                    pe.wait_ge(a_hT, g + 2)
                    qk(wk, 4, a_K, g + 2)
                if prev:
                    project(g)
                turn_p(g + 1)
                if prev:
                    pe.wait_ge(a_y, g)
                if nxt:
                    qk(wq, 6, a_Q, g + 2)
                    pe.wait_ge(a_k, 3 * (g + 2))
                pv(g + 1, 0)
                if nxt:
                    pe.wait_ge(a_q, 3 * (g + 2))
                pv(g + 1, 1)
                pe.wait_ge(a_o, 8 * g + 4)
                if nxt:
                    values(g + 2)
                if nxt2:
                    pe.wait_ge(a_o, 8 * g + 8)
                    turn(a_xn, a_T, g + 3, 6)

            step(0, False, True, True)
            with pe.Fori(1, NG - 2) as g:
                step(g, True, True, True)
            step(NG - 2, True, True, False)
            step(NG - 1, True, False, False)
            turn(m_xn, m_T, 1, 4)
            turn_out(NG)

            def hidden(u):
                pe.wait_ge(m_hT, u + 1)
                for j in range(5):
                    if j == 4:
                        pe.wait_ge(m_hx, 9 * u + 2)
                    for c in range(2 * j, min(2 * j + 2, NF)):
                        for k in range(NK):
                            ins = mm(ps[:, j % 4, 256 * (c % 2):256 * (c % 2) + 256],
                                     wf1[:, k, 128 * c:128 * c + 128], hT[:, k], k == 0, k == NK - 1)
                    ins.then_inc(m_F, 1)

            def down(n, by_pair=False):
                pe.wait_ge(m_g, n)
                for t in range(G):
                    if by_pair and t == 1:
                        pe.wait_ge(m_g, n + 1)
                    for c in range(NF):
                        ins = mm(ps[:, 6 + t, 0:C], hg[:, c, 128 * t:128 * t + 128], wf2[:, c], c == 0, c == NF - 1)
                    ins.then_inc(m_Y, 1)

            pe.wait_ge(ld_m, 16 * 4)

            def mstep(u, prev, nxt):
                if prev:
                    pe.wait_ge(m_hx, 9 * u)
                hidden(u)
                if nxt:
                    turn(m_xn, m_T, u + 2, 4)
                if prev:
                    down(u)
                else:
                    project(NG)

            mstep(0, False, True)
            with pe.Fori(1, NG - 1) as u:
                mstep(u, True, True)
            mstep(NG - 1, True, False)
            down(NG, by_pair=True)


def kernel(x, cond_1152, L0_cond_P, L0_cond_W, L0_cond_b, L1_cond_W_qkv, L1_cond_b_qkv, L1_cond_W_proj,
           L1_cond_b_proj, L1_cond_W_fc1, L1_cond_b_fc1, L1_cond_W_fc2, L1_cond_b_fc2, L1_cond_W_ada, L1_cond_b_ada):
    import concourse.bacc as bacc
    from concourse.bass_utils import run_bass_kernel_spmd

    def chunks(a):
        return a.reshape(NK, KC, -1).transpose(1, 0, 2)

    def rep(a, n):
        return np.tile(np.asarray(a)[None], (n,) + (1,) * np.asarray(a).ndim)

    def parities(a):
        return a.reshape(-1, 8, 2, DH).transpose(0, 2, 1, 3).reshape(-1, C)

    def head_rows(a):
        rows = np.zeros((HP, 3), np.float32)
        for c, (h0, h1) in enumerate(HEADS):
            rows[:DH * (h1 - h0), c] = a[DH * h0:DH * h1]
        return rows

    tokens = np.asarray(x).reshape(B * L, C)
    Wr, br = np.asarray(L0_cond_W), np.asarray(L0_cond_b)
    packed = np.zeros((D, D), np.int64)
    packed[np.triu_indices(D, 1)] = np.arange(D * (D - 1) // 2)
    fold_w = np.zeros((32, D, C), np.float32)
    fold_b = np.zeros((32, D), np.float32)
    for r in range(32):
        for c in range(D):
            if c != r:
                k = packed[r, c] if c > r else packed[32 + c, 32 + r]
                fold_w[r, c], fold_b[r, c] = Wr[k], br[k]
    Wqkv, bqkv = np.asarray(L1_cond_W_qkv), np.asarray(L1_cond_b_qkv)
    bada = np.asarray(L1_cond_b_ada).reshape(6, C)
    arrays = {
        "x": tokens,
        "xT": chunks(tokens.T),
        "condT": chunks(np.asarray(cond_1152).T),
        "PT": np.asarray(L0_cond_P).T,
        "Wfold": chunks(fold_w.reshape(2048, C).T),
        "bfold": fold_b.reshape(1, 2048),
        "Wada": chunks(np.asarray(L1_cond_W_ada)),
        "bada_col": bada[[0, 1, 3, 4]].reshape(4, NK, KC).transpose(2, 0, 1),
        "bada_gate": bada[[2, 5]][None],
        "Wq": chunks(Wqkv[:, 0:C]),
        "Wk": chunks(Wqkv[:, C:2 * C]),
        "bq": head_rows(bqkv[0:C]),
        "bk": head_rows(bqkv[C:2 * C]),
        "Wv": chunks(parities(Wqkv[:, 2 * C:])),
        "bv": parities(bqkv[None, 2 * C:]).reshape(2, 1, C // 2).repeat(L, axis=1).reshape(128, C // 2),
        "Wp": chunks(np.asarray(L1_cond_W_proj)),
        "bp": rep(L1_cond_b_proj, 128),
        "Wf1": chunks(np.asarray(L1_cond_W_fc1)),
        "bf1": np.asarray(L1_cond_b_fc1).reshape(NF, 128).T,
        "Wf2": np.asarray(L1_cond_W_fc2).reshape(NF, 128, C).transpose(1, 0, 2),
        "bf2": rep(L1_cond_b_fc2, 128),
        "consts": constants(),
    }
    nc = bacc.Bacc("TRN2", target_bir_lowering=False, num_devices=1)
    feed, args = {}, []
    for name, a in arrays.items():
        a = np.ascontiguousarray(a)
        feed[f"in_{name}"] = a
        args.append(nc.dram_tensor(f"in_{name}", a.shape, F32, kind="ExternalInput").ap())
    args.append(nc.dram_tensor("skew_scratch", (B, 2048), F32, kind="Internal").ap())
    args.append(nc.dram_tensor("gate_scratch", (B, 2, C), F32, kind="Internal").ap())
    args.append(nc.dram_tensor("out", (B * L, C), F32, kind="ExternalOutput").ap())
    cond_block_kernel(nc, *args)
    r = run_bass_kernel_spmd(nc, [feed], core_ids=[0])
    return r.results[0]["out"].reshape(B, L, C)
```
